# Optimizing a Trainium2 kernel written in Bass

```python
import numpy as np
import jax
import jax.numpy as jnp

def _softmax(x, axis=-1):
    return jax.nn.softmax(x, axis=axis)

def _gelu(x):
    return jax.nn.gelu(x, approximate=True)

def _silu(x):
    return jax.nn.silu(x)

def _sigmoid(x):
    return jax.nn.sigmoid(x)

def _layernorm(x, axis=-1, eps=1e-05):
    m = jnp.mean(x, axis=axis, keepdims=True)
    v = jnp.var(x, axis=axis, keepdims=True)
    return (x - m) / jnp.sqrt(v + eps)

def _scatter_add(tgt, idx, src, axis=0):
    return tgt.at[idx].add(src)

def _segment_sum(src, seg, n):
    return jax.ops.segment_sum(src, seg, n)
kernel_name = 'mk_vit_tower_d1_tok_img1024_r4_b50127'

def setup_inputs(seed: int=0):
    np.random.seed(seed)
    _w = jnp.asarray

    def _rec_inputs():
        import jax
        import jax.numpy as jnp
        _rk = jax.random.key(seed)
        x = -0.00016672 + 0.999947 * jax.random.normal(jax.random.fold_in(_rk, 1), (64, 3, 96, 96), jnp.float32)
        return x
    x = _rec_inputs()

    def _L0_tok_setup():
        import jax, jax.numpy as jnp
        import numpy as np
        P = 16

        def _patchify(x):
            B, C, H, W = x.shape
            gh, gw = (H // P, W // P)
            x = x.reshape(B, C, gh, P, gw, P)
            x = x.transpose(0, 2, 4, 1, 3, 5)
            return x.reshape(B, gh * gw, C * P * P)
        key = jax.random.key(seed)
        k1, k2, k3, k4, k5 = jax.random.split(key, 5)
        B, C, S = (64, 3, 96)
        lin_in, lout = (P * P * C, 256)
        n_patches = (S // P) ** 2
        return {'x': jax.random.normal(k1, (B, C, S, S), dtype=jnp.float32), 'W': jax.random.normal(k2, (lout, lin_in), dtype=jnp.float32) * 0.02, 'b': jax.random.normal(k3, (lout,), dtype=jnp.float32) * 0.02, 'class_token': jax.random.normal(k4, (1, 1, lout), dtype=jnp.float32) * 0.02, 'pos_embedding': jax.random.normal(k5, (1, n_patches + 1, lout), dtype=jnp.float32) * 0.02}
    _L0_tok_all = _L0_tok_setup()
    _L0_tok_in = {k: v for k, v in _L0_tok_all.items() if k in ('W', 'b', 'class_token', 'pos_embedding')}
    del _L0_tok_all

    def _L0_attn_setup():
        import jax, jax.numpy as jnp
        import numpy as np
        import math
        DIM = 256
        NUM_HEADS = 16
        HEAD_DIM = DIM // NUM_HEADS
        BATCH = 4
        SEQ = 1024

        def _feature_map(x, R):
            x = x / math.sqrt(HEAD_DIM)
            proj = jnp.einsum('bhnd,dm->bhnm', x, R)
            sq_norm = jnp.sum(x * x, axis=-1, keepdims=True)
            return jnp.exp(proj - 0.5 * sq_norm)
        key = jax.random.key(seed)
        ks = jax.random.split(key, 10)
        s = 1.0 / math.sqrt(DIM)
        return {'x': jax.random.normal(ks[0], (BATCH, SEQ, DIM), dtype=jnp.float32), 'Wq': jax.random.normal(ks[1], (DIM, DIM), dtype=jnp.float32) * s, 'bq': jax.random.normal(ks[2], (DIM,), dtype=jnp.float32) * 0.01, 'Wk': jax.random.normal(ks[3], (DIM, DIM), dtype=jnp.float32) * s, 'bk': jax.random.normal(ks[4], (DIM,), dtype=jnp.float32) * 0.01, 'Wv': jax.random.normal(ks[5], (DIM, DIM), dtype=jnp.float32) * s, 'bv': jax.random.normal(ks[6], (DIM,), dtype=jnp.float32) * 0.01, 'Wo': jax.random.normal(ks[7], (DIM, DIM), dtype=jnp.float32) * s, 'bo': jax.random.normal(ks[8], (DIM,), dtype=jnp.float32) * 0.01, 'R': jax.random.normal(ks[9], (HEAD_DIM, HEAD_DIM), dtype=jnp.float32) * 0.4}
    _L0_attn_all = _L0_attn_setup()
    _L0_attn_in = {k: v for k, v in _L0_attn_all.items() if k in ('Wq', 'bq', 'Wk', 'bk', 'Wv', 'bv', 'Wo', 'bo', 'R')}
    del _L0_attn_all

    def _L0_ffn_setup():
        import jax, jax.numpy as jnp
        import numpy as np
        B, T, D, F, E = (2, 256, 256, 1024, 8)
        EPS = 1e-06
        key = jax.random.key(seed)
        k = jax.random.split(key, 5)
        scale = 0.02
        return {'x': jax.random.normal(k[0], (B, T, D), dtype=jnp.float32), 'rms_w': jnp.ones((D,), dtype=jnp.float32), 'gate_w': jax.random.normal(k[1], (E, D), dtype=jnp.float32) * scale, 'W1': jax.random.normal(k[2], (E, D, F), dtype=jnp.float32) * scale, 'b1': jnp.zeros((E, F), dtype=jnp.float32), 'W2': jax.random.normal(k[3], (E, F, D), dtype=jnp.float32) * scale, 'b2': jnp.zeros((E, D), dtype=jnp.float32)}
    _L0_ffn_all = _L0_ffn_setup()
    _L0_ffn_in = {k: v for k, v in _L0_ffn_all.items() if k in ('rms_w', 'gate_w', 'W1', 'b1', 'W2', 'b2')}
    del _L0_ffn_all
    return {'x': x, 'L0_tok_W': _L0_tok_in['W'], 'L0_tok_b': _L0_tok_in['b'], 'L0_tok_class_token': _L0_tok_in['class_token'], 'L0_tok_pos_embedding': _L0_tok_in['pos_embedding'], 'L0_attn_Wq': _L0_attn_in['Wq'], 'L0_attn_bq': _L0_attn_in['bq'], 'L0_attn_Wk': _L0_attn_in['Wk'], 'L0_attn_bk': _L0_attn_in['bk'], 'L0_attn_Wv': _L0_attn_in['Wv'], 'L0_attn_bv': _L0_attn_in['bv'], 'L0_attn_Wo': _L0_attn_in['Wo'], 'L0_attn_bo': _L0_attn_in['bo'], 'L0_attn_R': _L0_attn_in['R'], 'L0_ffn_rms_w': _L0_ffn_in['rms_w'], 'L0_ffn_gate_w': _L0_ffn_in['gate_w'], 'L0_ffn_W1': _L0_ffn_in['W1'], 'L0_ffn_b1': _L0_ffn_in['b1'], 'L0_ffn_W2': _L0_ffn_in['W2'], 'L0_ffn_b2': _L0_ffn_in['b2']}

def reference(x, L0_tok_W, L0_tok_b, L0_tok_class_token, L0_tok_pos_embedding, L0_attn_Wq, L0_attn_bq, L0_attn_Wk, L0_attn_bk, L0_attn_Wv, L0_attn_bv, L0_attn_Wo, L0_attn_bo, L0_attn_R, L0_ffn_rms_w, L0_ffn_gate_w, L0_ffn_W1, L0_ffn_b1, L0_ffn_W2, L0_ffn_b2):
    import jax
    import jax.numpy as jnp

    def _L0_tok_ref(x, W, b, class_token, pos_embedding):
        import jax, jax.numpy as jnp
        import numpy as np
        P = 16

        def _patchify(x):
            B, C, H, W = x.shape
            gh, gw = (H // P, W // P)
            x = x.reshape(B, C, gh, P, gw, P)
            x = x.transpose(0, 2, 4, 1, 3, 5)
            return x.reshape(B, gh * gw, C * P * P)
        patches = _patchify(x)
        proj = jnp.einsum('bnk,dk->bnd', patches, W) + b
        B = x.shape[0]
        cls = jnp.broadcast_to(class_token, (B, 1, proj.shape[-1]))
        out = jnp.concatenate([cls, proj], axis=1) + pos_embedding
        return out

    def _L0_attn_ref(x, Wq, bq, Wk, bk, Wv, bv, Wo, bo, R):
        import jax, jax.numpy as jnp
        import numpy as np
        import math
        DIM = 256
        NUM_HEADS = 16
        HEAD_DIM = DIM // NUM_HEADS
        BATCH = 4
        SEQ = 1024

        def _feature_map(x, R):
            x = x / math.sqrt(HEAD_DIM)
            proj = jnp.einsum('bhnd,dm->bhnm', x, R)
            sq_norm = jnp.sum(x * x, axis=-1, keepdims=True)
            return jnp.exp(proj - 0.5 * sq_norm)
        b, n, _ = x.shape
        h, d = (NUM_HEADS, HEAD_DIM)

        def split_heads(t):
            return t.reshape(b, n, h, d).transpose(0, 2, 1, 3)
        q = split_heads(x @ Wq.T + bq)
        k = split_heads(x @ Wk.T + bk)
        v = split_heads(x @ Wv.T + bv)
        q_prime = _feature_map(q, R)
        k_prime = _feature_map(k, R)
        kv = jnp.einsum('bhnd,bhne->bhde', k_prime, v)
        z = 1.0 / (jnp.sum(q_prime, axis=-1) + 1e-08)
        out = jnp.einsum('bhnd,bhde,bhn->bhne', q_prime, kv, z)
        out = out.transpose(0, 2, 1, 3).reshape(b, n, DIM)
        return out @ Wo.T + bo

    def _L0_ffn_ref(x, rms_w, gate_w, W1, b1, W2, b2):
        import jax, jax.numpy as jnp
        import numpy as np
        B, T, D, F, E = (2, 256, 256, 1024, 8)
        EPS = 1e-06
        ms = jnp.mean(x * x, axis=-1, keepdims=True)
        xn = x * jax.lax.rsqrt(ms + EPS) * rms_w
        logits = jnp.einsum('btd,ed->bte', xn, gate_w)
        scores = jax.nn.softmax(logits, axis=-1)
        top1_idx = jnp.argmax(scores, axis=-1)
        top1_score = jnp.max(scores, axis=-1)
        out = jnp.zeros_like(xn)
        for e in range(E):
            h = jax.nn.silu(jnp.einsum('btd,df->btf', xn, W1[e]) + b1[e])
            ye = jnp.einsum('btf,fd->btd', h, W2[e]) + b2[e]
            out = jnp.where((top1_idx == e)[..., None], ye, out)
        return out * top1_score[..., None]
    h = _L0_tok_ref(x, L0_tok_W, L0_tok_b, L0_tok_class_token, L0_tok_pos_embedding)
    h = h + _L0_attn_ref(_layernorm(h, axis=-1), L0_attn_Wq, L0_attn_bq, L0_attn_Wk, L0_attn_bk, L0_attn_Wv, L0_attn_bv, L0_attn_Wo, L0_attn_bo, L0_attn_R)
    h = h + _L0_ffn_ref(_layernorm(h, axis=-1), L0_ffn_rms_w, L0_ffn_gate_w, L0_ffn_W1, L0_ffn_b1, L0_ffn_W2, L0_ffn_b2)
    return h

_drawn_inputs = setup_inputs


def setup_inputs(seed=0):
    import zlib

    import numpy as np

    out = dict(_drawn_inputs(seed))
    spreads = {'L0_ffn_rms_w': (1.0, 0.6), 'L0_ffn_b1': (0.0, 0.8), 'L0_ffn_b2': (0.0, 0.8)}
    factors = {'L0_attn_bq': 8.0,
     'L0_attn_bk': 8.0,
     'L0_attn_bo': 8.0,
     'L0_ffn_gate_w': 7.872,
     'L0_ffn_W1': 8.0,
     'L0_ffn_W2': 8.0}
    for name, (base, spread) in spreads.items():
        noise = np.random.default_rng([zlib.crc32(name.encode()), seed]).standard_normal(out[name].shape)
        drawn = base * np.exp(spread * noise) if base else spread * noise
        out[name] = jnp.asarray(drawn.astype(out[name].dtype))
    for name, factor in factors.items():
        out[name] = (out[name] * factor).astype(out[name].dtype)
    return out
```

```python
from contextlib import ExitStack

import concourse.bass as bass
from concourse import mybir

F32 = mybir.dt.float32
F32R = mybir.dt.float32r
I32 = mybir.dt.int32
ALU = mybir.AluOpType
ACT = mybir.ActivationFunctionType
AX = mybir.AxisListType

P = 128
IMGS, N = 64, 37
T = IMGS * N
NT = -(-T // P)
D = 256
KD = D // P
PIX = 768
KP = PIX // P
HD = 16
GI = 8
NG = IMGS // GI
GC = GI * N
SL = 64
NE, FF = 8, 1024
KF = FF // P
NS = (T + NE * (P - 1)) // P
LN_EPS, RMS_EPS, Z_EPS = 1e-5, 1e-6, 1e-8
KB = 1024


def pipeline(eng, n, skew, body, first=None):
    lo = first or (skew + 3) // 2 * 2
    hi = n // 2 * 2
    for i in range(lo):
        body(i, i % 2)
    with eng.Fori(lo // 2, hi // 2) as j:
        body(2 * j, 0)
        body(2 * j + 1, 1)
    for i in range(hi, n + skew):
        body(i, i % 2)


def inside(i, n):
    return not isinstance(i, int) or 0 <= i < n


def after(eng, sem, count):
    if not isinstance(count, int) or count > 0:
        eng.wait_ge(sem, count)


def settle(eng, sem, count, settled, value):
    eng.wait_ge(settled, value)
    eng.wait_ge(sem, count)


def vit_kernel(nc, xin, w_all, Rm, tok_b, cls_tok, pos, small_d, bo, W1, b1, W2, b2, consts, ids, out):
    with ExitStack() as ctx:
        def at(name, shape, dt, offset):
            return nc.alloc_sbuf_tensor_at(name, shape, dt, offset=offset)

        def sem(name):
            return ctx.enter_context(nc.semaphore(name))

        arena_bytes = 212832
        base = -(-nc.sbuf_base // 32) * 32
        ctx.enter_context(nc.sbuf_tensor("arena", [P, arena_bytes // 4], F32))

        class Region:
            def __init__(self, start, end):
                self.at, self.end = start, end

            def put(self, name, shape, dt):
                size = 4
                for s in shape[1:]:
                    size *= s
                size = -(-size // 32) * 32
                t = at(name, shape, dt, base + self.at)
                self.at += size
                assert self.at <= self.end, (name, self.at, self.end)
                return t

        EB = 4 * (KD * FF + KF * D)
        half = NE // 2 * EB
        wff = at("wff", [P, NE, KD * FF + KF * D], F32, base)
        low, mid, top = Region(0, half), Region(half, 2 * half), Region(2 * half, arena_bytes)

        WEMB = KP * D
        WQKV = 3 * KD * D
        w_raw = low.put("w_raw", [P, WEMB + WQKV + KD * D], F32)
        wemb_hi = low.put("wemb_hi", [P, KP, D], F32R)
        wemb_lo = low.put("wemb_lo", [P, KP, D], F32R)
        x_raw = [low.put(f"x_raw{p}", [P, KP + 1, P], F32) for p in range(2)]
        x_hi = [low.put(f"x_hi{p}", [P, KP + 1, P], F32R) for p in range(2)]
        x_lo = [low.put(f"x_lo{p}", [P, KP, P], F32R) for p in range(2)]
        xhat = [low.put(f"xhat{p}", [P, D], F32) for p in range(2)]
        tab_raw = low.put("tab_raw", [P, D], F32)
        tab_add = low.put("tab_add", [P, D], F32)
        tab = low.put("tab", [P, D], F32R)
        tab_tmp = low.put("tab_tmp", [P, D], F32R)
        xn_hi = mid.put("xn_hi", [P, KD, NT * P], F32R)
        xn_lo = mid.put("xn_lo", [P, KD, NT * P], F32R)
        wq_hi = mid.put("wq_hi", [P, 3, KD, D], F32R)
        wq_lo = mid.put("wq_lo", [P, 3, KD, D], F32R)
        s_q = mid.put("s_q", [P, KD, GC], F32)
        s_k = mid.put("s_k", [P, KD, GC], F32)
        kv_t = [mid.put(f"kv_t{r}", [P, 4 * P], F32) for r in range(2)]
        cst = top.put("cst", [P, 5 * P + 2], F32)
        ident, mask = cst[:, 0:P], cst[:, P:2 * P]
        upper, ones = cst[:, 2 * P:3 * P], cst[:, 3 * P:4 * P]
        iota = cst[:, 4 * P:5 * P]
        valid = cst[:, 5 * P:5 * P + 1]
        id1 = top.put("id1", [P, NT], F32)
        small = top.put("small", [P, (3 + 1 + NE) * KD], F32)
        b_c = small[:, 0:3 * KD].rearrange("p (a k) -> p a k", k=KD)
        rms_c = small[:, 3 * KD:4 * KD]
        gate_sb = small[:, 4 * KD:].rearrange("p (k e) -> p k e", k=KD)
        eps_ln = top.put("eps_ln", [P, 1], F32)
        eps_z = top.put("eps_z", [P, 1], F32)
        mv = top.put("mv", [P, NT, 2], F32)
        std = top.put("std", [P, NT], F32)
        rstd = top.put("rstd", [P, NT], F32)
        mvt = [top.put(f"mvt{p}", [P, 2], F32) for p in range(2)]
        bn = [top.put(f"bn{p}", [P, 6], F32) for p in range(2)]
        gidx = top.put("gidx", [P, NS], I32)
        sidx = top.put("sidx", [P, NS], I32)
        slot_score = top.put("slot_score", [P, NS], F32)
        gi = [top.put(f"gi{p}", [P, 1], I32) for p in range(2)]
        si = [top.put(f"si{p}", [P, 1], I32) for p in range(2)]
        spare = top.put("spare", [P, 1], F32)
        e_tile = top.put("e_tile", [P, NS], I32)
        ffn_start = top.at
        h_tok = top.put("h_tok", [P, NT, D], F32)
        outT = top.put("outT", [P, KD, NT * P], F32)
        wo_hi = top.put("wo_hi", [P, KD, D], F32R)
        wo_lo = top.put("wo_lo", [P, KD, D], F32R)
        bo_bc = top.put("bo_bc", [P, D], F32)
        ph2_start = top.at
        blk = top.put("blk", [P, P], F32)
        rbd_raw = top.put("rbd_raw", [P, P], F32)
        r_hi = top.put("r_hi", [P, P], F32R)
        r_lo = top.put("r_lo", [P, P], F32R)
        q_hi = top.put("q_hi", [P, KD, GC], F32R)
        q_lo = top.put("q_lo", [P, KD, GC], F32R)
        k_hi = top.put("k_hi", [P, KD, GC], F32R)
        k_lo = top.put("k_lo", [P, KD, GC], F32R)
        qp = [top.put(f"qp{p}", [P, KD, GC], F32) for p in range(2)]
        kp = [top.put(f"kp{p}", [P, KD, GI, SL], F32) for p in range(2)]
        low2 = Region(low.at, half)
        vt = [low2.put(f"vt{p}", [P, KD, GI, SL], F32) for p in range(2)]
        s_sb = low2.put("s_sb", [P, KD, GC], F32)
        kv_sb = Region(0, 14 * KB).put("kv_sb", [P, 2, 2, 4 * P], F32)
        top3 = Region(ph2_start, arena_bytes)
        oh = [top3.put(f"oh{p}", [P, KD, P], F32R) for p in range(2)]
        ol = [top3.put(f"ol{p}", [P, KD, P], F32R) for p in range(2)]
        h2_t = [top3.put(f"h2_t{p}", [P, D], F32) for p in range(2)]
        g_tok = [top3.put(f"g_tok{p}", [P, D], F32) for p in range(2)]
        gT = [top3.put(f"gT{p}", [P, KD, P], F32) for p in range(2)]
        R = NE * NT
        logit = top3.put("logit", [P, NE, NT], F32)
        onehot = top3.put("onehot", [P, NE, NT], F32)
        rt1 = top3.put("rt1", [P, NE, NT], F32)
        rt2 = top3.put("rt2", [P, NE, NT], F32)
        tot = top3.put("tot", [P, NE, NT], F32)
        mx = top3.put("mx", [P, NT], F32)
        t19 = [top3.put(f"t19_{i}", [P, NT], F32) for i in range(6)]
        slot_i = top3.put("slot_i", [P, NT], I32)
        st_i = top3.put("st_i", [P, NT], I32)
        sp_i = top3.put("sp_i", [P, NT], I32)
        t8 = [top3.put(f"t8_{i}", [P, NE], F32) for i in range(6)]
        t8i = top3.put("t8i", [P, NE], I32)
        t26 = [top3.put(f"t26_{i}", [P, NS], F32) for i in range(3)]
        cmp26 = top3.put("cmp26", [P, NS, NE], F32)
        st_hot = top3.put("st_hot", [P, NT, NS], F32)
        sc_hi = top3.put("sc_hi", [P, NT], F32R)
        payload = top3.put("payload", [P, NT, 3, NS], F32R)
        sp_hot = [top3.put(f"sp_hot{p}", [P, P], F32R) for p in range(2)]
        top4 = Region(ffn_start, arena_bytes)
        b1_bc = top4.put("b1_bc", [P, NE, FF], F32)
        b2_bc = top4.put("b2_bc", [P, NE, D], F32)
        row = [top4.put(f"row{p}", [P, 2 * D], F32) for p in range(2)]
        h2c = [top4.put(f"h2c{p}", [P, D], F32) for p in range(2)]
        xT = [top4.put(f"xT{p}", [P, KD, P], F32) for p in range(2)]
        act_f = [top4.put(f"act_f{p}", [P, FF], F32) for p in range(2)]
        actT = [top4.put(f"actT{p}", [P, KF, P], F32) for p in range(2)]
        y_sb = top4.put("y_sb", [P, D], F32)
        o_sb = [top4.put(f"o_sb{p}", [P, D], F32) for p in range(2)]

        bank = [ctx.enter_context(nc.psum_tensor(f"bank{i}", [P, 2, 512], F32)) for i in range(4)]

        def bk(i):
            return bank[i // 2][:, i % 2, :]

        rows_d = nc.dram_tensor("rows_scratch", [NT * P, 2 * D], F32).ap()
        out_rows = out.rearrange("b n d -> (b n) d")

        s = {}
        for name in (
            "w_in tab_in cst_in zeroed w_emb_hi w_emb_split w_hi w_split tab_sum tab_hi tab_lo tab_done blk_done rbd_zero r_in "
            "x_in0 x_in1 x_hi_ready x_lo_ready emb_mm h_ready bn_done var_ready std_ready rstd_ready xhat_ready "
            "xhat_T xn_hi_ready xn_lo_ready bo_added "
            "v_mm q_mm k_mm v_ready q_hi_ready q_lo_ready sq_ready k_hi_ready k_lo_ready sk_ready fq_mm fk_mm "
            "qp_ready kp_ready pair_T pair_ready kv_mm kv_ready z_ready s_mm o_mm s_copied out_ready "
            "oh_ready ol_ready wo_mm h2_ready h2_bn h2_mv h2_kept mv_ready batch g_ready g_saved0 g_saved1 h2_saved gT_mm gT_ready logits_mm "
            "rt rt_act rt_pe hot_ready hot_mm payload_ready table_mm tables "
            "wff_low wff_high bias_in "
            "gi_ready si_ready row_in0 row_in1 row_copied x_T xT_ready s1_mm pre_act act_ready act_T actT_a actT_b s2_mm y_ready o_ready "
            "o_saved0 o_saved1"
        ).split():
            s[name] = sem(name)
        S = type("S", (), s)
        x_in, g_saved = [S.x_in0, S.x_in1], [S.g_saved0, S.g_saved1]
        row_in, o_saved = [S.row_in0, S.row_in1], [S.o_saved0, S.o_saved1]

        block = ctx.enter_context(nc.Block())
        QC = WEMB + WQKV

        @block.sync
        def _(sp):
            sp.dma_start(w_raw[:, 0:WEMB], w_all[:, 0:WEMB]).then_inc(S.w_in, 16)
            for o in (0, 64):
                sp.dma_start(tab_raw[o:o + N, :], pos[0]).then_inc(S.tab_in, 16)
                sp.dma_start(tab_add[o:o + 1, :], cls_tok[0]).then_inc(S.tab_in, 16)
                sp.dma_start(tab_add[o + 1:o + N, :], tok_b[None, :].broadcast_to([N - 1, D])).then_inc(S.tab_in, 16)

            def load_x(i, p):
                after(sp, S.x_hi_ready, i - 1)
                after(sp, S.x_lo_ready, i - 1)
                sp.dma_start(x_raw[p][:], xin[bass.ds(i, 1)].rearrange("a p k t -> (a p) k t")
                             if not isinstance(i, int) else xin[i]).then_inc(x_in[p], 16)

            load_x(0, 0)
            sp.dma_start(cst[:], consts).then_inc(S.cst_in, 16)
            sp.dma_start(id1[:], ids).then_inc(S.cst_in, 16)
            sp.dma_start(small[:], small_d).then_inc(S.cst_in, 16)
            sp.dma_start(bo_bc[:], bo[None, :].broadcast_to([P, D])).then_inc(S.cst_in, 16)
            load_x(1, 1)
            sp.wait_ge(S.w_in, 16)
            sp.dma_start(w_raw[:, WEMB:], w_all[:, WEMB:]).then_inc(S.w_in, 16)
            sp.wait_ge(S.rbd_zero, 1)
            for h in range(P // HD):
                sp.dma_start(rbd_raw[h * HD:(h + 1) * HD, h * HD:(h + 1) * HD], Rm).then_inc(S.r_in, 16)
            with sp.Fori(1, NT // 2) as j:
                load_x(2 * j, 0)
                load_x(2 * j + 1, 1)
            load_x(NT - 1, (NT - 1) % 2)

            def load_expert(e, done):
                sp.dma_start(wff[:, e, 0:KD * FF].rearrange("p (k f) -> p k f", k=KD),
                             W1[e].rearrange("(k p) f -> p k f", p=P)).then_inc(done, 16)
                sp.dma_start(wff[:, e, KD * FF:].rearrange("p (k d) -> p k d", k=KF),
                             W2[e].rearrange("(k p) d -> p k d", p=P)).then_inc(done, 16)

            sp.wait_ge(S.out_ready, NG)
            for e in range(NE):
                load_expert(e, S.wff_low if e < NE // 2 else S.wff_high)

            sp.wait_ge(S.h2_kept, NT)
            sp.dma_start(rows_d[:, D:].rearrange("(i p) d -> p i d", p=P), h_tok[:]).then_inc(S.h2_saved, 16)

            def save_g(i, p):
                after(sp, S.g_ready, i + 1)
                sp.dma_start(rows_d[bass.ds(i * P, P), 0:D], g_tok[p][:]).then_inc(g_saved[p], 16)
            pipeline(sp, NT, 0, save_g)

            sp.wait_ge(S.h2_saved, 16)
            sp.wait_ge(S.g_saved0, 16 * ((NT + 1) // 2))
            sp.wait_ge(S.g_saved1, 16 * (NT // 2))
            sp.wait_ge(S.tables, 1)
            sp.dma_start(b1_bc[:], b1[None].broadcast_to([P, NE, FF])).then_inc(S.bias_in, 16)
            sp.dma_start(b2_bc[:], b2[None].broadcast_to([P, NE, D])).then_inc(S.bias_in, 16)

        @block.gpsimd
        def _(pool):
            nc.gpsimd.memset(rbd_raw[:], 0.0).then_inc(S.rbd_zero, 1)
            nc.gpsimd.memset(outT[:, :, T:], 0.0).then_inc(S.zeroed, 1)
            for p in range(2):
                nc.gpsimd.memset(kp[p][:, :, :, N:], 0.0).then_inc(S.zeroed, 1)
                nc.gpsimd.memset(vt[p][:, :, :, N:], 0.0).then_inc(S.zeroed, 1)
            nc.gpsimd.memset(eps_ln[:], LN_EPS).then_inc(S.zeroed, 1)
            nc.gpsimd.memset(spare[:], 0.0)
            nc.gpsimd.memset(eps_z[:], Z_EPS).then_inc(S.zeroed, 1)
            pool.wait_ge(S.w_in, 16)
            pool.wait_ge(S.w_emb_hi, 1)
            nc.gpsimd.tensor_tensor(wemb_lo[:].rearrange("p k d -> p (k d)"), w_raw[:, 0:WEMB],
                                    wemb_hi[:].rearrange("p k d -> p (k d)").bitcast(F32),
                                    ALU.subtract).then_inc(S.w_emb_split, 1)
            pool.wait_ge(S.cst_in, 64)

            def body(i, p):
                if inside(i, NT):
                    settle(pool, S.x_hi_ready, i + 1, S.cst_in, 64)
                    after(pool, S.emb_mm, i - 1)
                    nc.gpsimd.tensor_tensor(x_lo[p][:], x_raw[p][:, 0:KP, :], x_hi[p][:, 0:KP, :].bitcast(F32),
                                            ALU.subtract).then_inc(S.x_lo_ready, 1)
                j = i - 3
                if inside(j, NT):
                    settle(pool, S.xhat_ready, j + 1, S.cst_in, 64)
                    hj = h_tok[:, bass.ds(j, 1), :].rearrange("p a d -> p (a d)")
                    nc.gpsimd.tensor_tensor(hj, hj, bo_bc[:], ALU.add).then_inc(S.bo_added, 1)
            pipeline(pool, NT, 3, body)

            def low_out(i, p):
                if inside(i, NT):
                    settle(pool, S.oh_ready, i + 1, S.cst_in, 64)
                    after(pool, S.wo_mm, i - 1)
                    nc.gpsimd.tensor_tensor(ol[p][:], outT[:, :, bass.ds(i * P, P)], oh[p][:].bitcast(F32),
                                            ALU.subtract).then_inc(S.ol_ready, 1)
                j = i - 2
                if inside(j, NT):
                    settle(pool, S.h2_ready, j + 1, S.cst_in, 64)
                    nc.gpsimd.tensor_copy(h_tok[:, bass.ds(j, 1), :].rearrange("p a d -> p (a d)"),
                                          h2_t[p][:]).then_inc(S.h2_kept, 1)
            pipeline(pool, NT, 2, low_out)

            pool.wait_ge(S.tables, 1)
            pool.wait_ge(S.bias_in, 32)

            def gather(t, p):
                pool.wait_ge(S.tables, 1)
                after(pool, S.x_T, t - 1)
                after(pool, S.row_copied, t - 1)
                after(pool, row_in[p], 16 * (t // 2))
                nc.gpsimd.tensor_copy(gi[p][:], gidx[:, bass.ds(t, 1)]).then_inc(S.gi_ready, 1)
                pool.wait_ge(S.gi_ready, t + 1)
                nc.gpsimd.tensor_tensor(spare[:], spare[:], spare[:], ALU.add)
                nc.gpsimd.indirect_dma_start(
                    row[p][:], None, rows_d, bass.IndirectOffsetOnAxis(ap=gi[p][:, 0:1], axis=0)
                ).then_inc(row_in[p], 16)

            def scatter(t, p):
                settle(pool, S.o_ready, t + 1, S.tables, 1)
                after(pool, o_saved[p], 16 * (t // 2))
                nc.gpsimd.tensor_copy(si[p][:], sidx[:, bass.ds(t, 1)]).then_inc(S.si_ready, 1)
                pool.wait_ge(S.si_ready, t + 1)
                nc.gpsimd.tensor_tensor(spare[:], spare[:], spare[:], ALU.add)
                nc.gpsimd.indirect_dma_start(
                    out_rows, bass.IndirectOffsetOnAxis(ap=si[p][:, 0:1], axis=0), o_sb[p][:], None,
                    bounds_check=T - 1, oob_is_err=False).then_inc(o_saved[p], 16)

            def body4(t, p):
                if inside(t, NS):
                    gather(t, p)
                if inside(t - 3, NS):
                    scatter(t - 3, 1 - p)
            pipeline(pool, NS, 3, body4)
            pool.wait_ge(S.o_saved0, 16 * (NS // 2))
            pool.wait_ge(S.o_saved1, 16 * (NS // 2))

        @block.scalar
        def _(act):
            act.wait_ge(S.w_in, 16)
            nc.scalar.copy(wemb_hi[:].rearrange("p k d -> p (k d)"), w_raw[:, 0:WEMB]).then_inc(S.w_emb_hi, 1)
            act.wait_ge(S.zeroed, 7)

            def body(i, p):
                if inside(i, NT):
                    act.wait_ge(x_in[p], 16 * (i // 2 + 1))
                    after(act, S.emb_mm, i - 1)
                    nc.scalar.copy(x_hi[p][:], x_raw[p][:]).then_inc(S.x_hi_ready, 1)
                j = i - 1
                if inside(j, NT):
                    act.wait_ge(S.emb_mm, j + 1)
                    nc.scalar.copy(h_tok[:, bass.ds(j, 1), :].rearrange("p a d -> p (a d)"),
                                   bk(1 - p)[:, 0:D]).then_inc(S.h_ready, 1)
                j = i - 2
                if inside(j, NT):
                    act.wait_ge(S.var_ready, j + 1)
                    nc.scalar.activation(std[:, p:p + 1], mvt[p][:, 1:2], ACT.Sqrt,
                                         bias=eps_ln[:, 0:1]).then_inc(S.std_ready, 1)
                j = i - 3
                if inside(j, NT):
                    act.wait_ge(S.xhat_T, j + 1)
                    nc.scalar.copy(xn_hi[:, :, bass.ds(j * P, P)],
                                   bk(3 - p)[:, 0:D].rearrange("p (k t) -> p k t", k=KD)).then_inc(S.xn_hi_ready, 1)
                if isinstance(i, int) and i == 2:
                    act.wait_ge(S.w_in, 32)
                    nc.scalar.copy(wq_hi[:].rearrange("p a k d -> p (a k d)"), w_raw[:, WEMB:QC]).then_inc(S.w_hi, 1)
                    nc.scalar.copy(wo_hi[:].rearrange("p k d -> p (k d)"), w_raw[:, QC:]).then_inc(S.w_hi, 1)
                    act.wait_ge(S.r_in, 16 * (P // HD))
                    nc.scalar.mul(r_hi[:], rbd_raw[:], 0.25).then_inc(S.w_hi, 1)
            pipeline(act, NT, 3, body)

            def proj(g, mm, pair, hi, hi_ready, sq, sq_ready, bias_row, free):
                act.wait_ge(mm, g + 1)
                after(act, free, g)
                for m in range(KD):
                    ins = nc.scalar.activation(hi[:, m, :], bank[pair][:, m, 0:GC], ACT.Identity,
                                               bias=b_c[:, bias_row, m:m + 1])
                ins.then_inc(hi_ready, 1)
                for m in range(KD):
                    ins = nc.scalar.activation(sq[:, m, :], bank[pair][:, m, 0:GC], ACT.Square,
                                               bias=b_c[:, bias_row, m:m + 1])
                ins.then_inc(sq_ready, 1)

            def pairs(g, js):
                for j in js:
                    act.wait_ge(S.pair_T, 4 * g + j + 1)
                    after(act, S.kv_mm, 4 * g + j - 1)
                    nc.scalar.copy(kv_t[j % 2][:], bk(6 + j % 2)).then_inc(S.pair_ready, 1)

            def attend(g, p):
                if inside(g, NG):
                    proj(g, S.q_mm, 0, q_hi, S.q_hi_ready, s_q, S.sq_ready, 0, S.fq_mm)
                    proj(g, S.k_mm, 1, k_hi, S.k_hi_ready, s_k, S.sk_ready, 1, S.fk_mm)
                if inside(g - 1, NG):
                    pairs(g - 1, (0, 1))
                if inside(g, NG):
                    act.wait_ge(S.fq_mm, g + 1)
                    after(act, S.o_mm, g - 1)
                    nc.scalar.activation(qp[p][:], bank[0][:, :, 0:GC], ACT.Exp).then_inc(S.qp_ready, 1)
                if inside(g - 1, NG):
                    pairs(g - 1, (2, 3))
                if inside(g, NG):
                    act.wait_ge(S.fk_mm, g + 1)
                    after(act, S.kv_mm, 4 * (g - 1))
                    nc.scalar.activation(kp[p][:, :, :, 0:N], bank[1][:, :, 0:GC].rearrange("p m (b t) -> p m b t", b=GI),
                                         ACT.Exp).then_inc(S.kp_ready, 1)
                if inside(g - 1, NG):
                    act.wait_ge(S.s_mm, g)
                    after(act, S.out_ready, g - 1)
                    nc.scalar.activation(s_sb[:], bank[3][:, :, 0:GC], ACT.Identity, bias=eps_z[:, 0:1],
                                         scale=-2.0 * HD).then_inc(S.s_copied, 1)
            pipeline(act, NG, 1, attend, 2)

            def high_out(i, p):
                after(act, S.wo_mm, i - 1)
                nc.scalar.copy(oh[p][:], outT[:, :, bass.ds(i * P, P)]).then_inc(S.oh_ready, 1)
            act.wait_ge(S.out_ready, NG)
            pipeline(act, NT, 0, high_out)
            act.wait_ge(S.mv_ready, NT)
            nc.scalar.activation(std[:], mv[:, :, 1], ACT.Sqrt, bias=eps_ln[:, 0:1]).then_inc(S.rt_act, 1)
            act.wait_ge(S.batch, 3)
            nc.scalar.activation(std[:], t19[0][:], ACT.Sqrt).then_inc(S.rt_act, 1)

            def scale_gT(i, p):
                act.wait_ge(S.gT_mm, i + 1)
                after(act, S.logits_mm, i - 1)
                for k in range(KD):
                    ins = nc.scalar.mul(gT[p][:, k, :], bk(2 + p)[:, k * P:(k + 1) * P], rms_c[:, k:k + 1])
                ins.then_inc(S.gT_ready, 1)
            pipeline(act, NT, 0, scale_gT)
            act.wait_ge(S.rt, 5)
            nc.scalar.activation(rt2[:], rt1[:], ACT.Exp).then_inc(S.rt_act, 1)

            def body4(t, p):
                if inside(t, NS):
                    act.wait_ge(S.x_T, t + 1)
                    after(act, S.s1_mm, t - 1)
                    for k in range(KD):
                        ins = nc.scalar.mul(xT[p][:, k, :], bk(6)[:, k * P:(k + 1) * P], rms_c[:, k:k + 1])
                    ins.then_inc(S.xT_ready, 1)
                t, p = t - 1, 1 - p
                if inside(t, NS):
                    act.wait_ge(S.pre_act, t + 1)
                    nc.scalar.activation(act_f[p][:], act_f[p][:], ACT.Silu).then_inc(S.act_ready, 1)
                t, p = t - 1, 1 - p
                if inside(t, NS):
                    act.wait_ge(S.act_T, t + 1)
                    after(act, S.s2_mm, t - 1)
                    nc.scalar.copy(actT[p][:, 0:KF // 2, :].rearrange("p k t -> p (k t)"), bk(4)).then_inc(S.actT_a, 1)
            act.wait_ge(S.bias_in, 32)
            pipeline(act, NS, 2, body4)

        @block.vector
        def _(dve):
            V = nc.vector
            V.memset(tab[:].bitcast(F32), 0.0).then_inc(S.tab_done, 1)
            dve.wait_ge(S.tab_in, 96)
            for o in (0, 64):
                V.tensor_tensor(tab_raw[o:o + N, :], tab_raw[o:o + N, :], tab_add[o:o + N, :],
                                ALU.add).then_inc(S.tab_sum, 1)
            dve.wait_ge(S.tab_sum, 2)
            dve.wait_ge(S.tab_done, 1)
            V.tensor_copy(tab[0:N, :], tab_raw[0:N, :])
            V.tensor_copy(tab_tmp[64:64 + N, :], tab_raw[64:64 + N, :]).then_inc(S.tab_hi, 1)
            dve.wait_ge(S.tab_hi, 1)
            V.tensor_tensor(tab[64:64 + N, :], tab_raw[64:64 + N, :], tab_tmp[64:64 + N, :].bitcast(F32),
                            ALU.subtract).then_inc(S.tab_done, 1)
            dve.wait_ge(S.cst_in, 64)
            V.tensor_scalar(blk[:], mask, -0.5 / HD, None, ALU.mult).then_inc(S.blk_done, 1)

            def body(i, p):
                j = i - 1
                if inside(j, NT):
                    dve.wait_ge(S.h_ready, j + 1)
                    V.bn_stats(bn[1 - p][:], bk(1 - p)[:, 0:D]).then_inc(S.bn_done, 1)
                    settle(dve, S.bn_done, j + 1, S.cst_in, 64)
                    V.bn_aggr(mvt[1 - p][:], bn[1 - p][:]).then_inc(S.var_ready, 1)
                j = i - 2
                if inside(j, NT):
                    dve.wait_ge(S.std_ready, j + 1)
                    V.reciprocal(rstd[:, p:p + 1], std[:, p:p + 1]).then_inc(S.rstd_ready, 1)
                    dve.wait_ge(S.rstd_ready, j + 1)
                    after(dve, S.xhat_T, j - 1)
                    V.tensor_scalar(xhat[p][:], h_tok[:, bass.ds(j, 1), :].rearrange("p a d -> p (a d)"),
                                    mvt[p][:, 0:1], rstd[:, p:p + 1],
                                    ALU.subtract, ALU.mult).then_inc(S.xhat_ready, 1)
                j = i - 3
                if inside(j, NT):
                    dve.wait_ge(S.xn_hi_ready, j + 1)
                    V.tensor_tensor(xn_lo[:, :, bass.ds(j * P, P)],
                                    bk(3 - p)[:, 0:D].rearrange("p (k t) -> p k t", k=KD),
                                    xn_hi[:, :, bass.ds(j * P, P)].bitcast(F32), ALU.subtract).then_inc(S.xn_lo_ready, 1)
                if isinstance(i, int) and i == 2:
                    dve.wait_ge(S.w_hi, 3)
                    V.tensor_tensor(wq_lo[:].rearrange("p a k d -> p (a k d)"), w_raw[:, WEMB:QC],
                                    wq_hi[:].rearrange("p a k d -> p (a k d)").bitcast(F32), ALU.subtract)
                    V.tensor_tensor(wo_lo[:].rearrange("p k d -> p (k d)"), w_raw[:, QC:],
                                    wo_hi[:].rearrange("p k d -> p (k d)").bitcast(F32), ALU.subtract)
                    V.scalar_tensor_tensor(r_lo[:], rbd_raw[:], 0.25, r_hi[:].bitcast(F32), ALU.mult,
                                           ALU.subtract).then_inc(S.w_split, 1)
            pipeline(dve, NT, 3, body)

            def low_part(g, pair, bias_row, hi, hi_ready, other, lo, lo_ready, free):
                dve.wait_ge(hi_ready, g + 1)
                dve.wait_ge(other, g + 1)
                after(dve, free, g)
                for m in range(KD):
                    ins = V.scalar_tensor_tensor(lo[:, m, :], bank[pair][:, m, 0:GC], b_c[:, bias_row, m:m + 1],
                                                 hi[:, m, :].bitcast(F32), ALU.add, ALU.subtract)
                ins.then_inc(lo_ready, 1)

            def mask_kv(g, p, half_i):
                dve.wait_ge(S.kv_mm, 4 * g + 2 * half_i + 2)
                after(dve, S.o_mm, g)
                for u in range(2):
                    ins = V.tensor_tensor(kv_sb[:, half_i, u, :].rearrange("p (a c) -> p a c", a=4),
                                          bk(4 + u).rearrange("p (a c) -> p a c", a=4),
                                          mask[:, None, :].broadcast_to([P, 4, P]), ALU.mult)
                ins.then_inc(S.kv_ready, 1)

            def attend(g, p):
                if inside(g, NG):
                    dve.wait_ge(S.v_mm, g + 1)
                    after(dve, S.pair_T, 4 * (g - 1))
                    for m in range(KD):
                        ins = V.tensor_scalar(vt[p][:, m, :, 0:N], bank[2][:, m, 0:GC].rearrange("p (b t) -> p b t", b=GI), b_c[:, 2, m:m + 1], None, ALU.add)
                    ins.then_inc(S.v_ready, 1)
                    low_part(g, 0, 0, q_hi, S.q_hi_ready, S.sq_ready, q_lo, S.q_lo_ready, S.fq_mm)
                    low_part(g, 1, 1, k_hi, S.k_hi_ready, S.sk_ready, k_lo, S.k_lo_ready, S.fk_mm)
                if inside(g - 1, NG):
                    mask_kv(g - 1, 1 - p, 0)
                    mask_kv(g - 1, 1 - p, 1)
                    dve.wait_ge(S.s_copied, g)
                    V.reciprocal(s_sb[:], s_sb[:]).then_inc(S.z_ready, 1)
                    dve.wait_ge(S.z_ready, g)
                    dve.wait_ge(S.o_mm, g)
                    V.tensor_tensor(outT[:, :, bass.ds((g - 1) * GC, GC)], bank[2][:, :, 0:GC], s_sb[:],
                                    ALU.mult).then_inc(S.out_ready, 1)
            pipeline(dve, NG, 1, attend, 2)

            def resid(i, p):
                dve.wait_ge(S.wo_mm, i + 1)
                dve.wait_ge(S.bo_added, i + 1)
                hi_ = h_tok[:, bass.ds(i, 1), :].rearrange("p a d -> p (a d)")
                after(dve, S.h2_kept, i - 1)
                V.tensor_tensor(h2_t[p][:], bk(p)[:, 0:D], hi_, ALU.add).then_inc(S.h2_ready, 1)
                dve.wait_ge(S.h2_ready, i + 1)
                V.bn_stats(bn[p][:], h2_t[p][:]).then_inc(S.h2_bn, 1)
                settle(dve, S.h2_bn, i + 1, S.cst_in, 64)
                V.bn_aggr(mvt[p][:], bn[p][:]).then_inc(S.h2_mv, 1)
                dve.wait_ge(S.h2_mv, i + 1)
                V.tensor_copy(mv[:, bass.ds(i, 1), :].rearrange("p a s -> p (a s)"), mvt[p][:]).then_inc(S.mv_ready, 1)
            pipeline(dve, NT, 0, resid)

            steps = [0]

            def step(ins, name=None):
                steps[0] += 1
                ins.then_inc(S.batch, 1)
                dve.wait_ge(S.batch, steps[0])

            dve.wait_ge(S.rt_act, 1)
            step(V.reciprocal(rstd[:], std[:]))
            step(V.tensor_tensor(t19[1][:], rstd[:], rstd[:], ALU.mult))
            V.tensor_tensor(t19[0][:], t19[1][:], mv[:, :, 1], ALU.mult).then_inc(S.rt_pe, 1)
            dve.wait_ge(S.rt_pe, 1)
            step(V.tensor_scalar(t19[0][:], t19[0][:], RMS_EPS, None, ALU.add))
            dve.wait_ge(S.rt_act, 2)
            step(V.reciprocal(t19[2][:], std[:]))
            step(V.tensor_tensor(rstd[:], rstd[:], t19[2][:], ALU.mult))

            def norm2(i, p):
                after(dve, S.gT_mm, i - 1)
                after(dve, g_saved[p], 16 * (i // 2))
                V.tensor_scalar(g_tok[p][:], h_tok[:, bass.ds(i, 1), :].rearrange("p a d -> p (a d)"),
                                mv[:, bass.ds(i, 1), 0], rstd[:, bass.ds(i, 1)],
                                ALU.subtract, ALU.mult).then_inc(S.g_ready, 1)
            dve.wait_ge(S.h2_kept, NT)
            pipeline(dve, NT, 0, norm2)

            def it(x):
                return x[:, None, :].broadcast_to([P, NE, NT])

            def ex(x):
                return x[:, :, None].broadcast_to([P, NE, NT])
            tiles_last = "p e i -> p i e"
            count = [0]

            def rstep(ins):
                count[0] += 1
                ins.then_inc(S.rt, 1)
                dve.wait_ge(S.rt, count[0])

            dve.wait_ge(S.logits_mm, NT)
            rstep(V.tensor_copy(logit[:].rearrange(tiles_last), bk(4)[:, 0:R].rearrange("p (i e) -> p i e", e=NE)))
            rstep(V.tensor_reduce(mx[:], logit[:].rearrange(tiles_last), AX.X, ALU.max))
            rstep(V.tensor_tensor(onehot[:], logit[:], it(mx), ALU.is_equal))
            prio = iota[:, NE:0:-1]
            rstep(V.tensor_tensor(onehot[:], onehot[:], ex(prio), ALU.mult))
            rstep(V.tensor_tensor(rt1[:], logit[:], it(mx), ALU.subtract))
            rstep(V.tensor_reduce(t19[0][:], onehot[:].rearrange(tiles_last), AX.X, ALU.max))
            rstep(V.tensor_tensor(onehot[:], it(t19[0]), ex(prio), ALU.is_equal))
            rstep(V.tensor_scalar(onehot[:, :, NT - 1], onehot[:, :, NT - 1], valid, None, ALU.mult))
            dve.wait_ge(S.rt_act, 3)
            rstep(V.tensor_reduce(t19[1][:], rt2[:].rearrange(tiles_last), AX.X, ALU.add))
            rstep(V.reciprocal(t19[1][:], t19[1][:]))
            rstep(V.tensor_scalar(t19[1][:, NT - 1:NT], t19[1][:, NT - 1:NT], valid, None, ALU.mult))
            rstep(V.tensor_copy(sc_hi[:], t19[1][:]))
            rstep(V.tensor_tensor(t19[2][:], t19[1][:], sc_hi[:].bitcast(F32), ALU.subtract))
            dve.wait_ge(S.rt_pe, 2)
            rstep(V.tensor_copy(tot[:].rearrange("p e i -> p (e i)"), bk(6)[:, 0:R]))
            rstep(V.memset(rt2[:], 1.0))
            flat = "p e i -> p (e i)"
            rstep(V.tensor_tensor_scan(rt1[:].rearrange(flat), rt2[:].rearrange(flat), tot[:].rearrange(flat), 0.0,
                                       ALU.mult, ALU.add))
            rstep(V.tensor_tensor(tot[:], rt1[:], tot[:], ALU.subtract))
            rstep(V.tensor_tensor(t8[0][:], rt1[:, :, NT - 1], tot[:, :, 0], ALU.subtract))
            rstep(V.tensor_scalar(t8i[:], t8[0][:], float(P - 1), None, ALU.add))
            rstep(V.tensor_scalar(t8i[:], t8i[:], 7, None, ALU.arith_shift_right))
            rstep(V.tensor_copy(t8[1][:], t8i[:]))
            rstep(V.tensor_tensor_scan(t8[2][:], rt2[:, 0, 0:NE], t8[1][:], 0.0, ALU.mult, ALU.add))
            rstep(V.tensor_tensor(t8[3][:], t8[2][:], t8[1][:], ALU.subtract))
            rstep(V.scalar_tensor_tensor(t8[4][:], t8[3][:], float(P), tot[:, :, 0], ALU.mult, ALU.subtract))
            rstep(V.tensor_tensor(rt1[:].rearrange(flat), bk(5)[:, 0:R], tot[:].rearrange(flat), ALU.add))
            rstep(V.tensor_tensor(rt1[:], rt1[:], ex(t8[4]), ALU.add))
            rstep(V.tensor_tensor(rt1[:], rt1[:], onehot[:], ALU.mult))
            rstep(V.tensor_reduce(t19[3][:], rt1[:].rearrange(tiles_last), AX.X, ALU.add))
            rstep(V.tensor_copy(slot_i[:], t19[3][:]))
            rstep(V.tensor_scalar(st_i[:], slot_i[:], 7, None, ALU.arith_shift_right))
            rstep(V.tensor_scalar(sp_i[:], slot_i[:], P - 1, None, ALU.bitwise_and))
            rstep(V.tensor_copy(t19[4][:], st_i[:]))
            rstep(V.tensor_copy(t19[5][:], sp_i[:]))
            rstep(V.tensor_tensor(st_hot[:], iota[:, None, 0:NS].broadcast_to([P, NT, NS]),
                                  t19[4][:, :, None].broadcast_to([P, NT, NS]), ALU.is_equal))
            for c, val in enumerate((id1[:], sc_hi[:].bitcast(F32), t19[2][:])):
                V.tensor_tensor(payload[:, :, c, :], st_hot[:], val[:, :, None].broadcast_to([P, NT, NS]),
                                ALU.mult).then_inc(S.payload_ready, 1)

            def hot(i, p):
                after(dve, S.hot_mm, i - 1)
                V.tensor_scalar(sp_hot[p][:], iota, t19[5][:, bass.ds(i, 1)], None, ALU.is_equal).then_inc(S.hot_ready, 1)
            pipeline(dve, NT, 0, hot)
            rstep(V.tensor_tensor(cmp26[:], iota[:, 0:NS, None].broadcast_to([P, NS, NE]),
                                  t8[2][:, None, :].broadcast_to([P, NS, NE]), ALU.is_ge))
            rstep(V.tensor_reduce(t26[0][:], cmp26[:], AX.X, ALU.add))
            rstep(V.tensor_scalar(e_tile[:], t26[0][:], float(NE - 1), None, ALU.min))
            dve.wait_ge(S.hot_mm, NT)
            rstep(V.tensor_copy(t26[0][:], bk(7)[:, 0:NS]))
            rstep(V.tensor_scalar(t26[1][:], t26[0][:], -1.0, 0.0, ALU.add, ALU.max))
            rstep(V.tensor_copy(gidx[:], t26[1][:]))
            rstep(V.tensor_scalar(t26[1][:], t26[0][:], 0.0, 4096.0, ALU.is_equal, ALU.mult))
            rstep(V.scalar_tensor_tensor(sidx[:], t26[0][:], -1.0, t26[1][:], ALU.add, ALU.add))
            rstep(V.tensor_copy(t26[2][:], bk(7)[:, NS:2 * NS]))
            V.tensor_tensor(slot_score[:], bk(7)[:, 2 * NS:3 * NS], t26[2][:], ALU.add).then_inc(S.tables, 1)

            def body4(t, p):
                t, p = t - 1, 1 - p
                if inside(t, NS):
                    e = dve.value_load(e_tile[0:1, bass.ds(t, 1)], min_val=0, max_val=NE - 1)
                    dve.wait_ge(S.s1_mm, t + 1)
                    after(dve, S.act_T, t - 1)
                    V.tensor_tensor(act_f[p][:].rearrange("p (a f) -> p a f", a=2), bank[p][:],
                                    b1_bc[:, bass.ds(e, 1), :].rearrange("p a (b f) -> p (a b) f", b=2),
                                    ALU.add).then_inc(S.pre_act, 1)
                t, p = t - 1, 1 - p
                if inside(t, NS):
                    dve.wait_ge(S.act_T, t + 1)
                    after(dve, S.s2_mm, t - 1)
                    V.tensor_copy(actT[p][:, KF // 2:, :].rearrange("p k t -> p (k t)"), bk(5)).then_inc(S.actT_b, 1)
                    e = dve.value_load(e_tile[0:1, bass.ds(t, 1)], min_val=0, max_val=NE - 1)
                    dve.wait_ge(S.s2_mm, t + 1)
                    V.tensor_tensor(y_sb[:], bk(7)[:, 0:D], b2_bc[:, bass.ds(e, 1), :].rearrange("p a d -> p (a d)"),
                                    ALU.add).then_inc(S.y_ready, 1)
                    dve.wait_ge(S.y_ready, t + 1)
                    after(dve, o_saved[p], 16 * (t // 2))
                    V.scalar_tensor_tensor(o_sb[p][:], y_sb[:], slot_score[:, bass.ds(t, 1)], h2c[p][:],
                                           ALU.mult, ALU.add).then_inc(S.o_ready, 1)
                t = t + 2
                if inside(t, NS):
                    dve.wait_ge(row_in[p], 16 * (t // 2 + 1))
                    after(dve, S.o_ready, t - 1)
                    V.tensor_copy(h2c[p][:], row[p][:, D:]).then_inc(S.row_copied, 1)
            dve.wait_ge(S.bias_in, 32)
            pipeline(dve, NS, 2, body4)

        @block.tensor
        def _(pe):
            def mm(o, lhsT, rhs, first, last):
                return nc.tensor.matmul(o, lhsT, rhs, start=first, stop=last, skip_group_check=True)

            def mm3(o, w, x, first, last):
                mm(o, w[1], x[0], first, False)
                mm(o, w[0], x[1], False, False)
                return mm(o, w[0], x[0], False, last)

            pe.wait_ge(S.w_emb_split, 1)
            pe.wait_ge(S.tab_done, 2)

            def stage1(i, p):
                if inside(i, NT):
                    pe.wait_ge(S.x_lo_ready, i + 1)
                    after(pe, S.bn_done, i - 1)
                    mm(bk(p)[:, 0:D], x_hi[p][:, KP, :], tab[:], True, False)
                    for k in range(KP):
                        ins = mm3(bk(p)[:, 0:D], (x_hi[p][:, k, :], x_lo[p][:, k, :]),
                                  (wemb_hi[:, k, :], wemb_lo[:, k, :]), False, k == KP - 1)
                    ins.then_inc(S.emb_mm, 1)
                j = i - 2
                if inside(j, NT):
                    pe.wait_ge(S.xhat_ready, j + 1)
                    after(pe, S.xn_lo_ready, j - 1)
                    for k in range(KD):
                        ins = nc.tensor.transpose(bk(2 + p)[:, k * P:(k + 1) * P], xhat[p][:, k * P:(k + 1) * P], ident)
                    ins.then_inc(S.xhat_T, 1)
            pipeline(pe, NT, 2, stage1)

            def project(g, which, pair):
                for m in range(KD):
                    for k in range(KD):
                        ins = mm3(bank[pair][:, m, 0:GC],
                                  (wq_hi[:, which, k, m * P:(m + 1) * P], wq_lo[:, which, k, m * P:(m + 1) * P]),
                                  (xn_hi[:, k, bass.ds(g * GC, GC)], xn_lo[:, k, bass.ds(g * GC, GC)]),
                                  k == 0, k == KD - 1)
                return ins

            def feature(g, pair, hi, lo, sq):
                for m in range(KD):
                    mm3(bank[pair][:, m, 0:GC], (r_hi[:], r_lo[:]), (hi[:, m, :], lo[:, m, :]), True, False)
                    ins = mm(bank[pair][:, m, 0:GC], blk[:], sq[:, m, :], False, True)
                return ins

            def pair_T(g, p, j):
                pe.wait_ge(S.kp_ready, g + 1)
                pe.wait_ge(S.v_ready, g + 1)
                after(pe, S.pair_ready, 4 * g + j - 1)
                if j < 2:
                    after(pe, S.s_copied, g)
                o = bk(6 + j % 2)
                for c, buf in enumerate((vt[p], kp[p])):
                    for m in range(KD):
                        ins = nc.tensor.transpose(o[:, (2 * c + m) * P:(2 * c + m + 1) * P], buf[:, m, 2 * j:2 * j + 2, :].rearrange("p b t -> p (b t)"),
                                                  ident)
                ins.then_inc(S.pair_T, 1)

            def pair_kv(g, j):
                pe.wait_ge(S.pair_ready, 4 * g + j + 1)
                if j == 2:
                    pe.wait_ge(S.kv_ready, 2 * g + 1)
                for u in range(2):
                    for m in range(KD):
                        ins = mm(bk(4 + u)[:, ((j % 2) * 2 + m) * P:((j % 2) * 2 + m + 1) * P],
                                 kv_t[j % 2][64 * u:64 * u + N, (2 + m) * P:(3 + m) * P],
                                 kv_t[j % 2][64 * u:64 * u + N, m * P:(m + 1) * P], True, True)
                ins.then_inc(S.kv_mm, 1)

            def attend(g, p):
                if inside(g, NG):
                    after(pe, S.out_ready, g - 1)
                    project(g, 2, 2).then_inc(S.v_mm, 1)
                    after(pe, S.qp_ready, g)
                    project(g, 0, 0).then_inc(S.q_mm, 1)
                    after(pe, S.kp_ready, g)
                    project(g, 1, 1).then_inc(S.k_mm, 1)
                if inside(g - 1, NG):
                    if inside(g, NG):
                        pe.wait_ge(S.v_ready, g + 1)
                    else:
                        pe.wait_ge(S.out_ready, g - 1)
                    pair_T(g - 1, 1 - p, 0)
                    pair_T(g - 1, 1 - p, 1)
                    pair_kv(g - 1, 0)
                    pair_kv(g - 1, 1)
                if inside(g, NG):
                    pe.wait_ge(S.q_lo_ready, g + 1)
                    feature(g, 0, q_hi, q_lo, s_q).then_inc(S.fq_mm, 1)
                if inside(g - 1, NG):
                    pair_T(g - 1, 1 - p, 2)
                    pair_T(g - 1, 1 - p, 3)
                    pair_kv(g - 1, 2)
                    pair_kv(g - 1, 3)
                if inside(g, NG):
                    pe.wait_ge(S.k_lo_ready, g + 1)
                    feature(g, 1, k_hi, k_lo, s_k).then_inc(S.fk_mm, 1)
                h, ph = g - 1, 1 - p
                if inside(h, NG):
                    pe.wait_ge(S.pair_ready, 4 * g)
                    for m in range(KD):
                        ins = mm(bk(6 + m)[:, 0:GC], blk[:], qp[ph][:, m, :], True, True)
                    ins.then_inc(S.s_mm, 1)
                    pe.wait_ge(S.kv_ready, 2 * g)
                    for b in range(GI):
                        for m in range(KD):
                            c = (b // 2 % 2) * 2 * P + m * P
                            ins = mm(bk(4 + m)[:, b * N:(b + 1) * N], kv_sb[:, b // 4, b % 2, c:c + P],
                                     qp[ph][:, m, b * N:(b + 1) * N], True, True)
                    ins.then_inc(S.o_mm, 1)
            pe.wait_ge(S.w_split, 1)
            pe.wait_ge(S.blk_done, 1)
            pe.wait_ge(S.xn_lo_ready, NT)
            pipeline(pe, NG, 1, attend, 2)

            def wo(i, p):
                pe.wait_ge(S.ol_ready, i + 1)
                after(pe, S.h2_ready, i - 1)
                for m in range(KD):
                    ins = mm3(bk(p)[:, 0:D], (oh[p][:, m, :], ol[p][:, m, :]), (wo_hi[:, m, :], wo_lo[:, m, :]),
                              m == 0, m == KD - 1)
                ins.then_inc(S.wo_mm, 1)
            pipeline(pe, NT, 0, wo)

            def gate_tile(i, p):
                if inside(i, NT):
                    pe.wait_ge(S.g_ready, i + 1)
                    after(pe, S.gT_ready, i - 1)
                    for k in range(KD):
                        ins = nc.tensor.transpose(bk(2 + p)[:, k * P:(k + 1) * P], g_tok[p][:, k * P:(k + 1) * P], ident)
                    ins.then_inc(S.gT_mm, 1)
                j = i - 1
                if inside(j, NT):
                    pe.wait_ge(S.gT_ready, j + 1)
                    for k in range(KD):
                        ins = mm(bk(4)[:, bass.ds(j * NE, NE)], gT[1 - p][:, k, :], gate_sb[:, k, :], k == 0, k == KD - 1)
                    ins.then_inc(S.logits_mm, 1)
            pe.wait_ge(S.out_ready, NG)
            pipeline(pe, NT, 1, gate_tile)

            pe.wait_ge(S.rt, 8)
            mm(bk(5)[:, 0:R], upper, onehot[:].rearrange("p e i -> p (e i)"), True, True)
            mm(bk(6)[:, 0:R], ones, onehot[:].rearrange("p e i -> p (e i)"), True, True).then_inc(S.rt_pe, 1)
            pe.wait_ge(S.payload_ready, 3)

            def table(i, p):
                pe.wait_ge(S.hot_ready, i + 1)
                first = isinstance(i, int) and i == 0
                last = isinstance(i, int) and i == NT - 1
                mm(bk(7)[:, 0:3 * NS], sp_hot[p][:], payload[:, bass.ds(i, 1), :, :].rearrange("p a c s -> p (a c s)"),
                   first, last).then_inc(S.hot_mm, 1)
            pipeline(pe, NT, 0, table)

            def x_T(t, p):
                pe.wait_ge(row_in[p], 16 * (t // 2 + 1))
                after(pe, S.xT_ready, t)
                for k in range(KD):
                    ins = nc.tensor.transpose(bk(6)[:, k * P:(k + 1) * P], row[p][:, k * P:(k + 1) * P], ident)
                ins.then_inc(S.x_T, 1)

            def weights(e, start, n):
                return wff[:, bass.ds(e, 1), start:start + n].rearrange("p a n -> p (a n)")

            def body4(t, p):
                if inside(t, NS):
                    x_T(t, p)
                t, p = t - 1, 1 - p
                if inside(t, NS):
                    e = pe.value_load(e_tile[0:1, bass.ds(t, 1)], min_val=0, max_val=NE - 1)
                    pe.wait_ge(S.xT_ready, t + 1)
                    after(pe, S.pre_act, t - 1)
                    for f in range(2):
                        for k in range(KD):
                            ins = mm(bank[p][:, f, :], xT[p][:, k, :], weights(e, k * FF + f * 512, 512),
                                     k == 0, k == KD - 1)
                    ins.then_inc(S.s1_mm, 1)
                t, p = t - 1, 1 - p
                if inside(t, NS):
                    e = pe.value_load(e_tile[0:1, bass.ds(t, 1)], min_val=0, max_val=NE - 1)
                    pe.wait_ge(S.act_ready, t + 1)
                    after(pe, S.actT_a, t)
                    after(pe, S.actT_b, t)
                    for k in range(KF):
                        ins = nc.tensor.transpose(bk(4 + k // 4)[:, (k % 4) * P:(k % 4 + 1) * P],
                                                  act_f[p][:, k * P:(k + 1) * P], ident)
                    ins.then_inc(S.act_T, 1)
                    after(pe, S.o_ready, t)
                    pe.wait_ge(S.actT_a, t + 1)
                    for k in range(KF):
                        if k == KF // 2:
                            pe.wait_ge(S.actT_b, t + 1)
                        ins = mm(bk(7)[:, 0:D], actT[p][:, k, :], weights(e, KD * FF + k * D, D), k == 0, k == KF - 1)
                    ins.then_inc(S.s2_mm, 1)
            pe.wait_ge(S.bias_in, 32)
            pe.wait_ge(S.wff_low, 16 * NE)
            pe.wait_ge(S.wff_high, 16 * NE)
            pipeline(pe, NS, 2, body4)


def kernel(**inputs):
    import numpy as np
    import concourse.bacc as bacc
    from concourse.bass_utils import run_bass_kernel_spmd

    f = np.float32

    def blocks(w):
        k, m = w.shape
        return np.ascontiguousarray(w.reshape(k // P, P, m).transpose(1, 0, 2).reshape(P, -1))

    x = np.asarray(inputs["x"])
    patches = np.zeros((PIX, IMGS, N), x.dtype)
    patches[:, :, 1:] = x.reshape(IMGS, 3, 6, 16, 6, 16).transpose(1, 3, 5, 0, 2, 4).reshape(PIX, IMGS, N - 1)
    xin = np.zeros((NT, P, KP + 1, P), x.dtype)
    cols = np.zeros((PIX, NT * P), x.dtype)
    cols[:, :T] = patches.reshape(PIX, T)
    xin[:, :, :KP, :] = cols.reshape(KP, P, NT, P).transpose(2, 1, 0, 3)
    tok = np.arange(NT * P) % N
    sel = np.zeros((P, NT * P), f)
    sel[tok, np.arange(NT * P)] = 1
    sel[64 + tok, np.arange(NT * P)] = 1
    xin[:, :, KP, :] = sel.reshape(P, NT, P).transpose(1, 0, 2)

    w_all = np.concatenate([blocks(np.asarray(inputs[n]).T) for n in
                            ("L0_tok_W", "L0_attn_Wq", "L0_attn_Wk", "L0_attn_Wv", "L0_attn_Wo")], axis=1)
    head = np.arange(P) // HD
    consts = np.concatenate([
        np.eye(P, dtype=f), (head[:, None] == head[None, :]).astype(f),
        (np.arange(P)[:, None] < np.arange(P)[None, :]).astype(f), np.ones((P, P), f),
        np.tile(np.arange(P, dtype=f), (P, 1)),
        np.tile((np.arange(P) < T - (NT - 1) * P).astype(f)[:, None], (1, 2))], axis=1)
    number = np.arange(NT * P).reshape(NT, P).T
    ids = np.where(number < T, number + 1, 0).astype(f)
    small = np.concatenate([np.asarray(inputs[n]).reshape(KD, P).T for n in
                            ("L0_attn_bq", "L0_attn_bk", "L0_attn_bv", "L0_ffn_rms_w")]
                           + [blocks(np.asarray(inputs["L0_ffn_gate_w"]).T)], axis=1)
    arrays = {
        "xin": xin, "w_all": w_all, "Rm": inputs["L0_attn_R"], "tok_b": inputs["L0_tok_b"],
        "cls_tok": inputs["L0_tok_class_token"], "pos": inputs["L0_tok_pos_embedding"],
        "small": small, "bo": inputs["L0_attn_bo"],
        "W1": inputs["L0_ffn_W1"], "b1": inputs["L0_ffn_b1"], "W2": inputs["L0_ffn_W2"], "b2": inputs["L0_ffn_b2"],
        "consts": consts, "ids": ids,
    }
    arrays = {k: np.ascontiguousarray(v) for k, v in arrays.items()}
    nc = bacc.Bacc("TRN2", target_bir_lowering=False, num_devices=1)
    args = [nc.dram_tensor(k, v.shape, mybir.dt.from_np(v.dtype), kind="ExternalInput").ap() for k, v in arrays.items()]
    out = nc.dram_tensor("out", (IMGS, N, D), F32, kind="ExternalOutput").ap()
    vit_kernel(nc, *args, out)
    r = run_bass_kernel_spmd(nc, [arrays], core_ids=[0])
    return r.results[0]["out"]
```

```python
from contextlib import ExitStack

import concourse.bass as bass
from concourse import mybir

F32 = mybir.dt.float32
F32R = mybir.dt.float32r
I32 = mybir.dt.int32
ALU = mybir.AluOpType
ACT = mybir.ActivationFunctionType
AX = mybir.AxisListType

P = 128
IMGS, N = 64, 37
T = IMGS * N
NT = -(-T // P)
D = 256
KD = D // P
PIX = 768
KP = PIX // P
HD = 16
GI = 8
NG = IMGS // GI
GC = GI * N
SL = 64
NE, FF = 8, 1024
KF = FF // P
NS = (T + NE * (P - 1)) // P
LN_EPS, RMS_EPS, Z_EPS = 1e-5, 1e-6, 1e-8
KB = 1024


def pipeline(eng, n, skew, body, first=None, by=2):
    lo = first or (skew + 1 + by) // by * by
    hi = n // by * by
    for i in range(lo):
        body(i, i % by)
    with eng.Fori(lo // by, hi // by) as j:
        for u in range(by):
            body(by * j + u, u)
    for i in range(hi, n + skew):
        body(i, i % by)


def inside(i, n):
    return not isinstance(i, int) or 0 <= i < n


def after(eng, sem, count):
    if not isinstance(count, int) or count > 0:
        eng.wait_ge(sem, count)


def settle(eng, sem, count, settled, value):
    eng.wait_ge(settled, value)
    eng.wait_ge(sem, count)


def vit_kernel(nc, xin, w_all, Rm, tok_b, cls_tok, pos, small_d, bo, W1, b1, W2, b2, consts, ids, out):
    with ExitStack() as ctx:
        def at(name, shape, dt, offset):
            return nc.alloc_sbuf_tensor_at(name, shape, dt, offset=offset)

        def sem(name):
            return ctx.enter_context(nc.semaphore(name))

        arena_bytes = 212832
        base = -(-nc.sbuf_base // 32) * 32
        ctx.enter_context(nc.sbuf_tensor("arena", [P, arena_bytes // 4], F32))

        class Region:
            def __init__(self, start, end):
                self.at, self.end = start, end

            def put(self, name, shape, dt):
                size = 4
                for s in shape[1:]:
                    size *= s
                size = -(-size // 32) * 32
                t = at(name, shape, dt, base + self.at)
                self.at += size
                assert self.at <= self.end, (name, self.at, self.end)
                return t

        EB = 4 * (KD * FF + KF * D)
        wff = at("wff", [P, NE, KD * FF + KF * D], F32, base)
        WEMB = KP * D
        WQKV = 3 * KD * D
        top0 = NE * EB

        low = Region(0, 2 * EB)
        wemb_hi = low.put("wemb_hi", [P, KP, D], F32R)
        wemb_lo = low.put("wemb_lo", [P, KP, D], F32R)
        x_raw = [low.put(f"x_raw{p}", [P, KP + 1, P], F32) for p in range(2)]
        x_hi = [low.put(f"x_hi{p}", [P, KP + 1, P], F32R) for p in range(2)]
        xhat = [low.put(f"xhat{p}", [P, D], F32) for p in range(2)]
        mid = Region(2 * EB, 6 * EB)
        xn_hi = mid.put("xn_hi", [P, KD, NT * P], F32R)
        xn_lo = mid.put("xn_lo", [P, KD, NT * P], F32R)
        kv_t = [mid.put(f"kv_t{r}", [P, 4 * P], F32) for r in range(2)]
        vt = [mid.put(f"vt{p}", [P, KD, GI, SL], F32) for p in range(2)]
        s_sb = mid.put("s_sb", [P, KD, GC], F32)
        late1 = Region(6 * EB, top0)
        w_raw = late1.put("w_raw", [P, WEMB + WQKV + KD * D], F32)
        x_lo = [late1.put(f"x_lo{p}", [P, KP, P], F32R) for p in range(2)]
        tab_raw = late1.put("tab_raw", [P, D], F32)
        tab_add = late1.put("tab_add", [P, D], F32)
        tab = late1.put("tab", [P, D], F32R)
        tab_tmp = late1.put("tab_tmp", [P, D], F32R)
        late2 = Region(6 * EB, top0)
        outT = late2.put("outT", [P, KD, NT * P], F32)
        kv_sb = late2.put("kv_sb", [P, 2, 2, 4 * P], F32)
        top = Region(top0, arena_bytes)
        cst = top.put("cst", [P, 5 * P + 2], F32)
        ident, mask = cst[:, 0:P], cst[:, P:2 * P]
        upper, ones = cst[:, 2 * P:3 * P], cst[:, 3 * P:4 * P]
        iota = cst[:, 4 * P:5 * P]
        valid = cst[:, 5 * P:5 * P + 1]
        id1 = top.put("id1", [P, NT], F32)
        small = top.put("small", [P, (3 + 1 + NE) * KD], F32)
        b_c = small[:, 0:3 * KD].rearrange("p (a k) -> p a k", k=KD)
        rms_c = small[:, 3 * KD:4 * KD]
        gate_sb = small[:, 4 * KD:].rearrange("p (k e) -> p k e", k=KD)
        eps_ln = top.put("eps_ln", [P, 1], F32)
        eps_z = top.put("eps_z", [P, 1], F32)
        mv = top.put("mv", [P, NT, 2], F32)
        std = top.put("std", [P, NT], F32)
        rstd = top.put("rstd", [P, NT], F32)
        mvt = [top.put(f"mvt{p}", [P, 2], F32) for p in range(2)]
        bn = [top.put(f"bn{p}", [P, 6], F32) for p in range(2)]
        gidx = top.put("gidx", [P, NS], I32)
        sidx = top.put("sidx", [P, NS], I32)
        slot_score = top.put("slot_score", [P, NS], F32)
        gi = [top.put(f"gi{p}", [P, 1], I32) for p in range(2)]
        si = [top.put(f"si{p}", [P, 1], I32) for p in range(2)]
        spare = top.put("spare", [P, 1], F32)
        e_tile = top.put("e_tile", [P, NS], I32)
        t19_0 = top.put("t19_0", [P, NT], F32)
        t19_1 = top.put("t19_1", [P, NT], F32)
        t19_2 = top.put("t19_2", [P, NT], F32)
        h_start = top.at
        h_tok = top.put("h_tok", [P, NT, D], F32)
        bias_start = top.at
        b1_bc = top.put("b1_bc", [P, NE, FF], F32)
        b2_bc = top.put("b2_bc", [P, NE, D], F32)
        work_start = top.at
        ph2 = Region(bias_start, work_start)
        wq_hi = ph2.put("wq_hi", [P, 3, KD, D], F32R)
        wq_lo = ph2.put("wq_lo", [P, 3, KD, D], F32R)
        blk = ph2.put("blk", [P, P], F32)
        r_hi = ph2.put("r_hi", [P, P], F32R)
        r_lo = ph2.put("r_lo", [P, P], F32R)
        q_hi = ph2.put("q_hi", [P, KD, GC], F32R)
        q_lo = ph2.put("q_lo", [P, KD, GC], F32R)
        k_hi = ph2.put("k_hi", [P, KD, GC], F32R)
        k_lo = ph2.put("k_lo", [P, KD, GC], F32R)
        kp = [ph2.put(f"kp{p}", [P, KD, GI, SL], F32) for p in range(2)]
        s_q = ph2.put("s_q", [P, KD, GC], F32)
        work = Region(work_start, arena_bytes)
        wo_hi = work.put("wo_hi", [P, KD, D], F32R)
        wo_lo = work.put("wo_lo", [P, KD, D], F32R)
        bo_split = work.put("bo_split", [P, D], F32R)
        ones_r = work.put("ones_r", [P, P], F32R)
        work2 = Region(work.at, arena_bytes)
        rbd_raw = work2.put("rbd_raw", [P, P], F32)
        bo_raw = work2.put("bo_raw", [P, D], F32)
        bo_tmp = work2.put("bo_tmp", [P, D], F32R)
        qp = [work2.put("qp0", [P, KD, GC], F32), mid.put("qp1", [P, KD, GC], F32)]
        s_k = work2.put("s_k", [P, KD, GC], F32)
        work3 = Region(work.at, arena_bytes)
        oh = [work3.put(f"oh{p}", [P, KD, P], F32R) for p in range(4)]
        ol = [work3.put(f"ol{p}", [P, KD, P], F32R) for p in range(4)]
        work3b = Region(work.at, arena_bytes)
        g_tok = [work3b.put(f"g_tok{p}", [P, D], F32) for p in range(4)]
        gT = [work3b.put(f"gT{p}", [P, KD, P], F32) for p in range(2)]
        R = NE * NT
        rr = Region(h_start, bias_start)
        logit = rr.put("logit", [P, NE, NT], F32)
        onehot = rr.put("onehot", [P, NE, NT], F32)
        rt1 = rr.put("rt1", [P, NE, NT], F32)
        rt2 = rr.put("rt2", [P, NE, NT], F32)
        tot = rr.put("tot", [P, NE, NT], F32)
        mx = rr.put("mx", [P, NT], F32)
        t19 = [t19_0, t19_1, t19_2] + [rr.put(f"t19_{i}", [P, NT], F32) for i in range(3, 6)]
        slot_i = rr.put("slot_i", [P, NT], I32)
        st_i = rr.put("st_i", [P, NT], I32)
        sp_i = rr.put("sp_i", [P, NT], I32)
        t8 = [rr.put(f"t8_{i}", [P, NE], F32) for i in range(6)]
        t8i = rr.put("t8i", [P, NE], I32)
        t26 = [rr.put(f"t26_{i}", [P, NS], F32) for i in range(3)]
        cmp26 = rr.put("cmp26", [P, NS, NE], F32)
        st_hot = rr.put("st_hot", [P, NT, NS], F32)
        sc_hi = rr.put("sc_hi", [P, NT], F32R)
        payload = rr.put("payload", [P, NT, 3, NS], F32R)
        sp_hot = [rr.put(f"sp_hot{p}", [P, P], F32R) for p in range(2)]
        ffn_a, ffn_b = Region(h_start, bias_start), Region(work_start, arena_bytes)
        act_f = [ffn_a.put(f"act_f{p}", [P, FF], F32) for p in range(2)]
        actT = [ffn_a.put(f"actT{p}", [P, KF, P], F32) for p in range(2)]
        h2c = [ffn_a.put(f"h2c{p}", [P, D], F32) for p in range(2)]
        y_sb = ffn_a.put("y_sb", [P, D], F32)
        row = [ffn_b.put(f"row{p}", [P, 2 * D], F32) for p in range(2)]
        xT = [ffn_b.put(f"xT{p}", [P, KD, P], F32) for p in range(2)]
        o_sb = [ffn_b.put(f"o_sb{p}", [P, D], F32) for p in range(2)]

        bank = [ctx.enter_context(nc.psum_tensor(f"bank{i}", [P, 2, 512], F32)) for i in range(4)]

        def bk(i):
            return bank[i // 2][:, i % 2, :]

        rows_d = nc.dram_tensor("rows_scratch", [NT * P, 2 * D], F32).ap()
        out_rows = out.rearrange("b n d -> (b n) d")

        s = {}
        for name in (
            "w_in tab_in cst_in zeroed w_emb_hi w_emb_split w_hi w_split tab_sum tab_hi tab_lo tab_done blk_done rbd_zero r_in "
            "x_in0 x_in1 x_hi_ready x_lo_ready emb_half emb_mm h_ready bn_done var_ready std_ready rstd_ready xhat_ready "
            "xhat_T xn_hi_ready xn_lo_ready tail_zero bo_hi bo_ready "
            "v_mm q_mm k_mm v_ready q_hi_ready q_lo_ready sq_ready k_hi_ready k_lo_ready sk_ready fq_mm fk_mm "
            "qp_ready kp_ready pair_T pair_ready kv_mm kv_ready z_ready s_mm o_mm s_copied out_ready "
            "oh_ready ol_ready wo_mm h2_bn h2_mv h2_kept mv_ready batch g_ready g_saved0 g_saved1 g_saved2 g_saved3 h2_saved gT_mm gT_ready logits_mm "
            "rt rt_act rt_pe hot_ready hot_mm payload_ready table_mm tables "
            "wff_in bias_in "
            "gi_ready si_ready row_in0 row_in1 row_copied x_T xT_ready s1_mm pre_act act_ready act_T actT_a actT_b s2_mm y_ready o_ready "
            "o_saved0 o_saved1"
        ).split():
            s[name] = sem(name)
        S = type("S", (), s)
        x_in, g_saved = [S.x_in0, S.x_in1], [S.g_saved0, S.g_saved1, S.g_saved2, S.g_saved3]
        row_in, o_saved = [S.row_in0, S.row_in1], [S.o_saved0, S.o_saved1]

        block = ctx.enter_context(nc.Block())
        QC = WEMB + WQKV
        CST = 16 * 5
        HB = KP // 2

        @block.sync
        def _(sp):
            sp.dma_start(w_raw[:, 0:WEMB], w_all[:, 0:WEMB]).then_inc(S.w_in, 16)
            for o in (0, 64):
                sp.dma_start(tab_raw[o:o + N, :], pos[0]).then_inc(S.tab_in, 16)
                sp.dma_start(tab_add[o:o + 1, :], cls_tok[0]).then_inc(S.tab_in, 16)
                sp.dma_start(tab_add[o + 1:o + N, :], tok_b[None, :].broadcast_to([N - 1, D])).then_inc(S.tab_in, 16)

            def load_x(i, p):
                after(sp, S.x_lo_ready, 2 * (i - 1))
                sp.dma_start(x_raw[p][:], xin[bass.ds(i, 1)].rearrange("a p k t -> (a p) k t")
                             if not isinstance(i, int) else xin[i]).then_inc(x_in[p], 16)

            load_x(0, 0)
            sp.dma_start(cst[:], consts).then_inc(S.cst_in, 16)
            sp.dma_start(id1[:], ids).then_inc(S.cst_in, 16)
            sp.dma_start(small[:], small_d).then_inc(S.cst_in, 16)
            for o in (0, 64):
                sp.dma_start(bo_raw[o:o + 1, :], bo[None, :]).then_inc(S.cst_in, 16)
            load_x(1, 1)
            sp.wait_ge(S.w_in, 16)
            sp.dma_start(w_raw[:, WEMB:], w_all[:, WEMB:]).then_inc(S.w_in, 16)
            sp.wait_ge(S.rbd_zero, 1)
            for h in range(P // HD):
                sp.dma_start(rbd_raw[h * HD:(h + 1) * HD, h * HD:(h + 1) * HD], Rm).then_inc(S.r_in, 16)
            with sp.Fori(1, NT // 2) as j:
                load_x(2 * j, 0)
                load_x(2 * j + 1, 1)
            load_x(NT - 1, (NT - 1) % 2)

            def load_expert(e, done):
                sp.dma_start(wff[:, e, 0:KD * FF].rearrange("p (k f) -> p k f", k=KD),
                             W1[e].rearrange("(k p) f -> p k f", p=P)).then_inc(done, 16)
                sp.dma_start(wff[:, e, KD * FF:].rearrange("p (k d) -> p k d", k=KF),
                             W2[e].rearrange("(k p) d -> p k d", p=P)).then_inc(done, 16)

            sp.wait_ge(S.xn_lo_ready, NT)
            load_expert(0, S.wff_in)
            load_expert(1, S.wff_in)
            sp.wait_ge(S.out_ready, NG)
            for e in range(2, 5):
                load_expert(e, S.wff_in)
            for i in range(0, NT, 4):
                n = min(4, NT - i)
                sp.wait_ge(S.h2_kept, i + n)
                sp.dma_start(rows_d[i * P:(i + n) * P, D:].rearrange("(i p) d -> p i d", p=P),
                             h_tok[:, i:i + n, :]).then_inc(S.h2_saved, 16)
            for e in range(NE):
                sp.wait_ge(S.g_ready, 2 * e + 2)
                sp.dma_start(b1_bc[:, e, :], b1[e:e + 1, :].broadcast_to([P, FF])).then_inc(S.bias_in, 16)
            sp.wait_ge(S.ol_ready, NT)
            for e in range(5, NE):
                load_expert(e, S.wff_in)
            sp.dma_start(b2_bc[:], b2[None].broadcast_to([P, NE, D])).then_inc(S.bias_in, 16)

        @block.gpsimd
        def _(pool):
            nc.gpsimd.memset(rbd_raw[:], 0.0).then_inc(S.rbd_zero, 1)
            for p in range(2):
                nc.gpsimd.memset(kp[p][:, :, :, N:], 0.0).then_inc(S.zeroed, 1)
                nc.gpsimd.memset(vt[p][:, :, :, N:], 0.0).then_inc(S.zeroed, 1)
            nc.gpsimd.memset(eps_ln[:], LN_EPS).then_inc(S.zeroed, 1)
            nc.gpsimd.memset(spare[:], 0.0)
            nc.gpsimd.memset(eps_z[:], Z_EPS).then_inc(S.zeroed, 1)
            pool.wait_ge(S.w_in, 16)
            pool.wait_ge(S.w_emb_hi, 1)
            nc.gpsimd.tensor_tensor(wemb_lo[:].rearrange("p k d -> p (k d)"), w_raw[:, 0:WEMB],
                                    wemb_hi[:].rearrange("p k d -> p (k d)").bitcast(F32),
                                    ALU.subtract).then_inc(S.w_emb_split, 1)
            pool.wait_ge(S.cst_in, CST)

            def body(i, p):
                for h in range(2):
                    settle(pool, S.x_hi_ready, 2 * i + h + 1, S.cst_in, CST)
                    after(pool, S.emb_mm if h else S.emb_half, i - 1)
                    ks = slice(h * HB, h * HB + HB)
                    nc.gpsimd.tensor_tensor(x_lo[p][:, ks, :], x_raw[p][:, ks, :], x_hi[p][:, ks, :].bitcast(F32),
                                            ALU.subtract).then_inc(S.x_lo_ready, 1)
            pipeline(pool, NT, 0, body)
            pool.wait_ge(S.xn_lo_ready, NT)
            nc.gpsimd.memset(outT[:, :, T:], 0.0).then_inc(S.tail_zero, 1)

            def low_out(i, p):
                settle(pool, S.oh_ready, i + 1, S.cst_in, CST)
                after(pool, S.wo_mm, i - 3)
                nc.gpsimd.tensor_tensor(ol[p][:], outT[:, :, bass.ds(i * P, P)], oh[p][:].bitcast(F32),
                                        ALU.subtract).then_inc(S.ol_ready, 1)
            pipeline(pool, NT, 0, low_out, by=4)

            def save_g(i, p):
                pool.wait_ge(S.g_ready, i + 1)
                pool.dma_start(rows_d[bass.ds(i * P, P), 0:D], g_tok[p][:]).then_inc(g_saved[p], 16)
            pipeline(pool, NT, 0, save_g, by=4)

            pool.wait_ge(S.tables, 1)
            pool.wait_ge(S.h2_saved, 16 * 5)
            for p in range(4):
                pool.wait_ge(g_saved[p], 16 * len(range(p, NT, 4)))

            def gather(t, p):
                pool.wait_ge(S.tables, 1)
                after(pool, S.x_T, t - 1)
                after(pool, S.row_copied, t - 1)
                after(pool, row_in[p], 16 * (t // 2))
                nc.gpsimd.tensor_copy(gi[p][:], gidx[:, bass.ds(t, 1)]).then_inc(S.gi_ready, 1)
                pool.wait_ge(S.gi_ready, t + 1)
                nc.gpsimd.tensor_tensor(spare[:], spare[:], spare[:], ALU.add)
                nc.gpsimd.indirect_dma_start(
                    row[p][:], None, rows_d, bass.IndirectOffsetOnAxis(ap=gi[p][:, 0:1], axis=0)
                ).then_inc(row_in[p], 16)

            def scatter(t, p):
                settle(pool, S.o_ready, t + 1, S.tables, 1)
                after(pool, o_saved[p], 16 * (t // 2))
                nc.gpsimd.tensor_copy(si[p][:], sidx[:, bass.ds(t, 1)]).then_inc(S.si_ready, 1)
                pool.wait_ge(S.si_ready, t + 1)
                nc.gpsimd.tensor_tensor(spare[:], spare[:], spare[:], ALU.add)
                nc.gpsimd.indirect_dma_start(
                    out_rows, bass.IndirectOffsetOnAxis(ap=si[p][:, 0:1], axis=0), o_sb[p][:], None,
                    bounds_check=T - 1, oob_is_err=False).then_inc(o_saved[p], 16)

            def body4(t, p):
                if inside(t, NS):
                    gather(t, p)
                if inside(t - 3, NS):
                    scatter(t - 3, 1 - p)
            pipeline(pool, NS, 3, body4)
            pool.wait_ge(S.o_saved0, 16 * (NS // 2))
            pool.wait_ge(S.o_saved1, 16 * (NS // 2))

        @block.scalar
        def _(act):
            act.wait_ge(S.w_in, 16)
            nc.scalar.copy(wemb_hi[:].rearrange("p k d -> p (k d)"), w_raw[:, 0:WEMB]).then_inc(S.w_emb_hi, 1)
            act.wait_ge(S.zeroed, 6)

            def body(i, p):
                if inside(i, NT):
                    act.wait_ge(x_in[p], 16 * (i // 2 + 1))
                    for h in range(2):
                        after(act, S.emb_mm if h else S.emb_half, i - 1)
                        ks = slice(HB, KP + 1) if h else slice(0, HB)
                        nc.scalar.copy(x_hi[p][:, ks, :], x_raw[p][:, ks, :]).then_inc(S.x_hi_ready, 1)
                j = i - 2
                if inside(j, NT):
                    act.wait_ge(S.var_ready, j + 1)
                    nc.scalar.activation(std[:, p:p + 1], mvt[p][:, 1:2], ACT.Sqrt,
                                         bias=eps_ln[:, 0:1]).then_inc(S.std_ready, 1)
                j = i - 3
                if inside(j, NT):
                    act.wait_ge(S.xhat_T, j + 1)
                    nc.scalar.copy(xn_hi[:, :, bass.ds(j * P, P)],
                                   bk(3 - p)[:, 0:D].rearrange("p (k t) -> p k t", k=KD)).then_inc(S.xn_hi_ready, 1)
                if isinstance(i, int) and i == 2:
                    act.wait_ge(S.w_in, 32)
                    nc.scalar.copy(wq_hi[:].rearrange("p a k d -> p (a k d)"), w_raw[:, WEMB:QC]).then_inc(S.w_hi, 1)
                    nc.scalar.copy(wo_hi[:].rearrange("p k d -> p (k d)"), w_raw[:, QC:]).then_inc(S.w_hi, 1)
                    act.wait_ge(S.r_in, 16 * (P // HD))
                    nc.scalar.mul(r_hi[:], rbd_raw[:], 0.25).then_inc(S.w_hi, 1)
            pipeline(act, NT, 3, body)

            def proj(g, mm, pair, hi, hi_ready, sq, sq_ready, bias_row, free):
                act.wait_ge(mm, g + 1)
                after(act, free, g)
                for m in range(KD):
                    ins = nc.scalar.activation(hi[:, m, :], bank[pair][:, m, 0:GC], ACT.Identity,
                                               bias=b_c[:, bias_row, m:m + 1])
                ins.then_inc(hi_ready, 1)
                for m in range(KD):
                    ins = nc.scalar.activation(sq[:, m, :], bank[pair][:, m, 0:GC], ACT.Square,
                                               bias=b_c[:, bias_row, m:m + 1])
                ins.then_inc(sq_ready, 1)

            def pairs(g, js):
                for j in js:
                    act.wait_ge(S.pair_T, 4 * g + j + 1)
                    after(act, S.kv_mm, 4 * g + j - 1)
                    nc.scalar.copy(kv_t[j % 2][:], bk(6 + j % 2)).then_inc(S.pair_ready, 1)

            def attend(i, p):
                g, h = i, i - 1
                if inside(h, NG):
                    act.wait_ge(S.s_mm, h + 1)
                    after(act, S.out_ready, h)
                    nc.scalar.activation(s_sb[:], bank[3][:, :, 0:GC], ACT.Identity, bias=eps_z[:, 0:1],
                                         scale=-2.0 * HD).then_inc(S.s_copied, 1)
                    pairs(h, (0, 1))
                if inside(g, NG):
                    proj(g, S.q_mm, 0, q_hi, S.q_hi_ready, s_q, S.sq_ready, 0, S.fq_mm)
                    proj(g, S.k_mm, 1, k_hi, S.k_hi_ready, s_k, S.sk_ready, 1, S.fk_mm)
                if inside(h, NG):
                    pairs(h, (2, 3))
                if inside(g, NG):
                    act.wait_ge(S.fq_mm, g + 1)
                    after(act, S.o_mm, g - 1)
                    nc.scalar.activation(qp[p][:], bank[0][:, :, 0:GC], ACT.Exp).then_inc(S.qp_ready, 1)
                    act.wait_ge(S.fk_mm, g + 1)
                    after(act, S.kv_mm, 4 * (g - 1))
                    nc.scalar.activation(kp[p][:, :, :, 0:N], bank[1][:, :, 0:GC].rearrange("p m (b t) -> p m b t", b=GI),
                                         ACT.Exp).then_inc(S.kp_ready, 1)
            pipeline(act, NG, 1, attend, 2)

            def high_out(i, p):
                if inside(i, NT):
                    after(act, S.wo_mm, i - 3)
                    nc.scalar.copy(oh[p][:], outT[:, :, bass.ds(i * P, P)]).then_inc(S.oh_ready, 1)
                j = i - 2
                if inside(j, NT):
                    act.wait_ge(S.h2_bn, j + 1)
                    nc.scalar.copy(h_tok[:, bass.ds(j, 1), :].rearrange("p a d -> p (a d)"),
                                   bk((p + 2) % 4)[:, 0:D]).then_inc(S.h2_kept, 1)
            act.wait_ge(S.out_ready, NG)
            act.wait_ge(S.tail_zero, 1)
            pipeline(act, NT, 2, high_out, 4, 4)
            act.wait_ge(S.mv_ready, NT)
            nc.scalar.activation(std[:], mv[:, :, 1], ACT.Sqrt, bias=eps_ln[:, 0:1]).then_inc(S.rt_act, 1)
            act.wait_ge(S.batch, 3)
            nc.scalar.activation(std[:], t19[0][:], ACT.Sqrt).then_inc(S.rt_act, 1)

            def scale_gT(i, p):
                act.wait_ge(S.gT_mm, i + 1)
                after(act, S.logits_mm, i - 1)
                for k in range(KD):
                    ins = nc.scalar.mul(gT[p][:, k, :], bk(2 + p)[:, k * P:(k + 1) * P], rms_c[:, k:k + 1])
                ins.then_inc(S.gT_ready, 1)
            pipeline(act, NT, 0, scale_gT)
            act.wait_ge(S.rt, 5)
            nc.scalar.activation(rt2[:], rt1[:], ACT.Exp).then_inc(S.rt_act, 1)

            def body4(t, p):
                if inside(t, NS):
                    act.wait_ge(S.x_T, t + 1)
                    after(act, S.s1_mm, t - 1)
                    for k in range(KD):
                        ins = nc.scalar.mul(xT[p][:, k, :], bk(6)[:, k * P:(k + 1) * P], rms_c[:, k:k + 1])
                    ins.then_inc(S.xT_ready, 1)
                t = t - 2
                if inside(t, NS):
                    act.wait_ge(S.act_T, t + 1)
                    after(act, S.s2_mm, t - 1)
                    nc.scalar.copy(actT[p][:, 0:KF // 2, :].rearrange("p k t -> p (k t)"), bk(4)).then_inc(S.actT_a, 1)
                t, p = t + 1, 1 - p
                if inside(t, NS):
                    act.wait_ge(S.pre_act, t + 1)
                    nc.scalar.activation(act_f[p][:], act_f[p][:], ACT.Silu).then_inc(S.act_ready, 1)
            act.wait_ge(S.tables, 1)
            pipeline(act, NS, 2, body4)

        @block.vector
        def _(dve):
            V = nc.vector
            V.memset(tab[:].bitcast(F32), 0.0).then_inc(S.tab_done, 1)
            dve.wait_ge(S.tab_in, 96)
            for o in (0, 64):
                V.tensor_tensor(tab_raw[o:o + N, :], tab_raw[o:o + N, :], tab_add[o:o + N, :],
                                ALU.add).then_inc(S.tab_sum, 1)
            dve.wait_ge(S.tab_sum, 2)
            dve.wait_ge(S.tab_done, 1)
            V.tensor_copy(tab[0:N, :], tab_raw[0:N, :])
            V.tensor_copy(tab_tmp[64:64 + N, :], tab_raw[64:64 + N, :]).then_inc(S.tab_hi, 1)
            dve.wait_ge(S.tab_hi, 1)
            V.tensor_tensor(tab[64:64 + N, :], tab_raw[64:64 + N, :], tab_tmp[64:64 + N, :].bitcast(F32),
                            ALU.subtract).then_inc(S.tab_done, 1)
            dve.wait_ge(S.cst_in, CST)
            V.tensor_scalar(blk[:], mask, -0.5 / HD, None, ALU.mult).then_inc(S.blk_done, 1)

            def body(i, p):
                j = i - 1
                if inside(j, NT):
                    dve.wait_ge(S.emb_mm, j + 1)
                    V.tensor_copy(h_tok[:, bass.ds(j, 1), :].rearrange("p a d -> p (a d)"),
                                  bk(1 - p)[:, 0:D]).then_inc(S.h_ready, 1)
                    V.bn_stats(bn[1 - p][:], bk(1 - p)[:, 0:D]).then_inc(S.bn_done, 1)
                    settle(dve, S.bn_done, j + 1, S.cst_in, CST)
                    V.bn_aggr(mvt[1 - p][:], bn[1 - p][:]).then_inc(S.var_ready, 1)
                j = i - 2
                if inside(j, NT):
                    dve.wait_ge(S.std_ready, j + 1)
                    V.reciprocal(rstd[:, p:p + 1], std[:, p:p + 1]).then_inc(S.rstd_ready, 1)
                    dve.wait_ge(S.rstd_ready, j + 1)
                    dve.wait_ge(S.h_ready, j + 1)
                    after(dve, S.xhat_T, j - 1)
                    V.tensor_scalar(xhat[p][:], h_tok[:, bass.ds(j, 1), :].rearrange("p a d -> p (a d)"),
                                    mvt[p][:, 0:1], rstd[:, p:p + 1],
                                    ALU.subtract, ALU.mult).then_inc(S.xhat_ready, 1)
                j = i - 3
                if inside(j, NT):
                    dve.wait_ge(S.xn_hi_ready, j + 1)
                    V.tensor_tensor(xn_lo[:, :, bass.ds(j * P, P)],
                                    bk(3 - p)[:, 0:D].rearrange("p (k t) -> p k t", k=KD),
                                    xn_hi[:, :, bass.ds(j * P, P)].bitcast(F32), ALU.subtract).then_inc(S.xn_lo_ready, 1)
                if isinstance(i, int) and i == 2:
                    dve.wait_ge(S.w_hi, 3)
                    V.tensor_tensor(wq_lo[:].rearrange("p a k d -> p (a k d)"), w_raw[:, WEMB:QC],
                                    wq_hi[:].rearrange("p a k d -> p (a k d)").bitcast(F32), ALU.subtract)
                    V.tensor_tensor(wo_lo[:].rearrange("p k d -> p (k d)"), w_raw[:, QC:],
                                    wo_hi[:].rearrange("p k d -> p (k d)").bitcast(F32), ALU.subtract)
                    V.scalar_tensor_tensor(r_lo[:], rbd_raw[:], 0.25, r_hi[:].bitcast(F32), ALU.mult,
                                           ALU.subtract).then_inc(S.w_split, 1)
                    V.tensor_copy(ones_r[:], ones)
                    V.memset(bo_split[:].bitcast(F32), 0.0).then_inc(S.bo_hi, 1)
                    dve.wait_ge(S.bo_hi, 1)
                    V.tensor_copy(bo_split[0:1, :], bo_raw[0:1, :])
                    V.tensor_copy(bo_tmp[64:65, :], bo_raw[64:65, :]).then_inc(S.bo_hi, 1)
                    dve.wait_ge(S.bo_hi, 2)
                    V.tensor_tensor(bo_split[64:65, :], bo_raw[64:65, :], bo_tmp[64:65, :].bitcast(F32),
                                    ALU.subtract).then_inc(S.bo_ready, 1)
            pipeline(dve, NT, 3, body)

            def low_part(g, pair, bias_row, hi, hi_ready, other, lo, lo_ready, free):
                dve.wait_ge(hi_ready, g + 1)
                dve.wait_ge(other, g + 1)
                after(dve, free, g)
                for m in range(KD):
                    ins = V.scalar_tensor_tensor(lo[:, m, :], bank[pair][:, m, 0:GC], b_c[:, bias_row, m:m + 1],
                                                 hi[:, m, :].bitcast(F32), ALU.add, ALU.subtract)
                ins.then_inc(lo_ready, 1)

            def mask_kv(g, p, half_i):
                dve.wait_ge(S.kv_mm, 4 * g + 2 * half_i + 2)
                after(dve, S.o_mm, g)
                for u in range(2):
                    ins = V.tensor_tensor(kv_sb[:, half_i, u, :].rearrange("p (a c) -> p a c", a=4),
                                          bk(4 + u).rearrange("p (a c) -> p a c", a=4),
                                          mask[:, None, :].broadcast_to([P, 4, P]), ALU.mult)
                ins.then_inc(S.kv_ready, 1)

            def attend(i, p):
                g, h = i, i - 1
                if inside(h, NG):
                    dve.wait_ge(S.s_copied, h + 1)
                    V.reciprocal(s_sb[:], s_sb[:]).then_inc(S.z_ready, 1)
                if inside(g, NG):
                    dve.wait_ge(S.v_mm, g + 1)
                    after(dve, S.pair_T, 4 * (g - 1))
                    for m in range(KD):
                        ins = V.tensor_scalar(vt[p][:, m, :, 0:N], bank[2][:, m, 0:GC].rearrange("p (b t) -> p b t", b=GI), b_c[:, 2, m:m + 1], None, ALU.add)
                    ins.then_inc(S.v_ready, 1)
                    low_part(g, 0, 0, q_hi, S.q_hi_ready, S.sq_ready, q_lo, S.q_lo_ready, S.fq_mm)
                if inside(h, NG):
                    mask_kv(h, 1 - p, 0)
                if inside(g, NG):
                    low_part(g, 1, 1, k_hi, S.k_hi_ready, S.sk_ready, k_lo, S.k_lo_ready, S.fk_mm)
                if inside(h, NG):
                    mask_kv(h, 1 - p, 1)
                    dve.wait_ge(S.z_ready, h + 1)
                    dve.wait_ge(S.o_mm, h + 1)
                    V.tensor_tensor(outT[:, :, bass.ds(h * GC, GC)], bank[2][:, :, 0:GC], s_sb[:],
                                    ALU.mult).then_inc(S.out_ready, 1)
            pipeline(dve, NG, 1, attend, 2)

            def stats(i, p):
                dve.wait_ge(S.wo_mm, i + 1)
                V.bn_stats(bn[p % 2][:], bk(p)[:, 0:D]).then_inc(S.h2_bn, 1)
                settle(dve, S.h2_bn, i + 1, S.cst_in, CST)
                V.bn_aggr(mvt[p % 2][:], bn[p % 2][:]).then_inc(S.h2_mv, 1)
                dve.wait_ge(S.h2_mv, i + 1)
                V.tensor_copy(mv[:, bass.ds(i, 1), :].rearrange("p a s -> p (a s)"), mvt[p % 2][:]).then_inc(S.mv_ready, 1)
            pipeline(dve, NT, 0, stats, by=4)

            steps = [0]

            def step(ins, name=None):
                steps[0] += 1
                ins.then_inc(S.batch, 1)
                dve.wait_ge(S.batch, steps[0])

            dve.wait_ge(S.rt_act, 1)
            step(V.reciprocal(rstd[:], std[:]))
            step(V.tensor_tensor(t19[1][:], rstd[:], rstd[:], ALU.mult))
            V.tensor_tensor(t19[0][:], t19[1][:], mv[:, :, 1], ALU.mult).then_inc(S.rt_pe, 1)
            dve.wait_ge(S.rt_pe, 1)
            step(V.tensor_scalar(t19[0][:], t19[0][:], RMS_EPS, None, ALU.add))
            dve.wait_ge(S.rt_act, 2)
            step(V.reciprocal(t19[2][:], std[:]))
            step(V.tensor_tensor(rstd[:], rstd[:], t19[2][:], ALU.mult))

            def norm2(i, p):
                after(dve, S.gT_mm, i - 3)
                after(dve, g_saved[p], 16 * (i // 4))
                V.tensor_scalar(g_tok[p][:], h_tok[:, bass.ds(i, 1), :].rearrange("p a d -> p (a d)"),
                                mv[:, bass.ds(i, 1), 0], rstd[:, bass.ds(i, 1)],
                                ALU.subtract, ALU.mult).then_inc(S.g_ready, 1)
            dve.wait_ge(S.h2_kept, NT)
            pipeline(dve, NT, 0, norm2, by=4)

            def it(x):
                return x[:, None, :].broadcast_to([P, NE, NT])

            def ex(x):
                return x[:, :, None].broadcast_to([P, NE, NT])
            tiles_last = "p e i -> p i e"
            count = [0]

            def rstep(ins):
                count[0] += 1
                ins.then_inc(S.rt, 1)
                dve.wait_ge(S.rt, count[0])

            dve.wait_ge(S.h2_saved, 16 * 5)
            dve.wait_ge(S.logits_mm, NT)
            rstep(V.tensor_copy(logit[:].rearrange(tiles_last), bk(4)[:, 0:R].rearrange("p (i e) -> p i e", e=NE)))
            rstep(V.tensor_reduce(mx[:], logit[:].rearrange(tiles_last), AX.X, ALU.max))
            rstep(V.tensor_tensor(onehot[:], logit[:], it(mx), ALU.is_equal))
            prio = iota[:, NE:0:-1]
            rstep(V.tensor_tensor(onehot[:], onehot[:], ex(prio), ALU.mult))
            rstep(V.tensor_tensor(rt1[:], logit[:], it(mx), ALU.subtract))
            rstep(V.tensor_reduce(t19[0][:], onehot[:].rearrange(tiles_last), AX.X, ALU.max))
            rstep(V.tensor_tensor(onehot[:], it(t19[0]), ex(prio), ALU.is_equal))
            rstep(V.tensor_scalar(onehot[:, :, NT - 1], onehot[:, :, NT - 1], valid, None, ALU.mult))
            dve.wait_ge(S.rt_act, 3)
            rstep(V.tensor_reduce(t19[1][:], rt2[:].rearrange(tiles_last), AX.X, ALU.add))
            rstep(V.reciprocal(t19[1][:], t19[1][:]))
            rstep(V.tensor_scalar(t19[1][:, NT - 1:NT], t19[1][:, NT - 1:NT], valid, None, ALU.mult))
            rstep(V.tensor_copy(sc_hi[:], t19[1][:]))
            rstep(V.tensor_tensor(t19[2][:], t19[1][:], sc_hi[:].bitcast(F32), ALU.subtract))
            dve.wait_ge(S.rt_pe, 2)
            rstep(V.tensor_copy(tot[:].rearrange("p e i -> p (e i)"), bk(6)[:, 0:R]))
            rstep(V.memset(rt2[:], 1.0))
            flat = "p e i -> p (e i)"
            rstep(V.tensor_tensor_scan(rt1[:].rearrange(flat), rt2[:].rearrange(flat), tot[:].rearrange(flat), 0.0,
                                       ALU.mult, ALU.add))
            rstep(V.tensor_tensor(tot[:], rt1[:], tot[:], ALU.subtract))
            rstep(V.tensor_tensor(t8[0][:], rt1[:, :, NT - 1], tot[:, :, 0], ALU.subtract))
            rstep(V.tensor_scalar(t8i[:], t8[0][:], float(P - 1), None, ALU.add))
            rstep(V.tensor_scalar(t8i[:], t8i[:], 7, None, ALU.arith_shift_right))
            rstep(V.tensor_copy(t8[1][:], t8i[:]))
            rstep(V.tensor_tensor_scan(t8[2][:], rt2[:, 0, 0:NE], t8[1][:], 0.0, ALU.mult, ALU.add))
            rstep(V.tensor_tensor(t8[3][:], t8[2][:], t8[1][:], ALU.subtract))
            rstep(V.scalar_tensor_tensor(t8[4][:], t8[3][:], float(P), tot[:, :, 0], ALU.mult, ALU.subtract))
            rstep(V.tensor_tensor(rt1[:].rearrange(flat), bk(5)[:, 0:R], tot[:].rearrange(flat), ALU.add))
            rstep(V.tensor_tensor(rt1[:], rt1[:], ex(t8[4]), ALU.add))
            rstep(V.tensor_tensor(rt1[:], rt1[:], onehot[:], ALU.mult))
            rstep(V.tensor_reduce(t19[3][:], rt1[:].rearrange(tiles_last), AX.X, ALU.add))
            rstep(V.tensor_copy(slot_i[:], t19[3][:]))
            rstep(V.tensor_scalar(st_i[:], slot_i[:], 7, None, ALU.arith_shift_right))
            rstep(V.tensor_scalar(sp_i[:], slot_i[:], P - 1, None, ALU.bitwise_and))
            rstep(V.tensor_copy(t19[4][:], st_i[:]))
            rstep(V.tensor_copy(t19[5][:], sp_i[:]))
            rstep(V.tensor_tensor(st_hot[:], iota[:, None, 0:NS].broadcast_to([P, NT, NS]),
                                  t19[4][:, :, None].broadcast_to([P, NT, NS]), ALU.is_equal))
            for c, val in enumerate((id1[:], sc_hi[:].bitcast(F32), t19[2][:])):
                V.tensor_tensor(payload[:, :, c, :], st_hot[:], val[:, :, None].broadcast_to([P, NT, NS]),
                                ALU.mult).then_inc(S.payload_ready, 1)

            def hot(i, p):
                after(dve, S.hot_mm, i - 1)
                V.tensor_scalar(sp_hot[p][:], iota, t19[5][:, bass.ds(i, 1)], None, ALU.is_equal).then_inc(S.hot_ready, 1)
            pipeline(dve, NT, 0, hot)
            rstep(V.tensor_tensor(cmp26[:], iota[:, 0:NS, None].broadcast_to([P, NS, NE]),
                                  t8[2][:, None, :].broadcast_to([P, NS, NE]), ALU.is_ge))
            rstep(V.tensor_reduce(t26[0][:], cmp26[:], AX.X, ALU.add))
            rstep(V.tensor_scalar(e_tile[:], t26[0][:], float(NE - 1), None, ALU.min))
            dve.wait_ge(S.hot_mm, NT)
            rstep(V.tensor_copy(t26[0][:], bk(7)[:, 0:NS]))
            rstep(V.tensor_scalar(t26[1][:], t26[0][:], -1.0, 0.0, ALU.add, ALU.max))
            rstep(V.tensor_copy(gidx[:], t26[1][:]))
            rstep(V.tensor_scalar(t26[1][:], t26[0][:], 0.0, 4096.0, ALU.is_equal, ALU.mult))
            rstep(V.scalar_tensor_tensor(sidx[:], t26[0][:], -1.0, t26[1][:], ALU.add, ALU.add))
            rstep(V.tensor_copy(t26[2][:], bk(7)[:, NS:2 * NS]))
            V.tensor_tensor(slot_score[:], bk(7)[:, 2 * NS:3 * NS], t26[2][:], ALU.add).then_inc(S.tables, 1)

            def body4(i, p):
                t = i - 2
                if inside(t, NS):
                    dve.wait_ge(S.act_T, t + 1)
                    after(dve, S.s2_mm, t - 1)
                    V.tensor_copy(actT[p][:, KF // 2:, :].rearrange("p k t -> p (k t)"), bk(5)).then_inc(S.actT_b, 1)
                t, r = i - 1, 1 - p
                if inside(t, NS):
                    e = dve.value_load(e_tile[0:1, bass.ds(t, 1)], min_val=0, max_val=NE - 1)
                    dve.wait_ge(S.s1_mm, t + 1)
                    after(dve, S.act_T, t - 1)
                    V.tensor_tensor(act_f[r][:].rearrange("p (a f) -> p a f", a=2), bank[r][:],
                                    b1_bc[:, bass.ds(e, 1), :].rearrange("p a (b f) -> p (a b) f", b=2),
                                    ALU.add).then_inc(S.pre_act, 1)
                t = i - 2
                if inside(t, NS):
                    e = dve.value_load(e_tile[0:1, bass.ds(t, 1)], min_val=0, max_val=NE - 1)
                    dve.wait_ge(S.s2_mm, t + 1)
                    V.tensor_tensor(y_sb[:], bk(7)[:, 0:D], b2_bc[:, bass.ds(e, 1), :].rearrange("p a d -> p (a d)"),
                                    ALU.add).then_inc(S.y_ready, 1)
                    dve.wait_ge(S.y_ready, t + 1)
                    after(dve, o_saved[p], 16 * (t // 2))
                    V.scalar_tensor_tensor(o_sb[p][:], y_sb[:], slot_score[:, bass.ds(t, 1)], h2c[p][:],
                                           ALU.mult, ALU.add).then_inc(S.o_ready, 1)
                if inside(i, NS):
                    dve.wait_ge(row_in[p], 16 * (i // 2 + 1))
                    after(dve, S.o_ready, i - 1)
                    V.tensor_copy(h2c[p][:], row[p][:, D:]).then_inc(S.row_copied, 1)
            dve.wait_ge(S.bias_in, 16 * (NE + 1))
            pipeline(dve, NS, 2, body4)

        @block.tensor
        def _(pe):
            def mm(o, lhsT, rhs, first, last):
                return nc.tensor.matmul(o, lhsT, rhs, start=first, stop=last, skip_group_check=True)

            def mm3(o, w, x, first, last):
                mm(o, w[1], x[0], first, False)
                mm(o, w[0], x[1], False, False)
                return mm(o, w[0], x[0], False, last)

            pe.wait_ge(S.w_emb_split, 1)
            pe.wait_ge(S.tab_done, 2)

            def stage1(i, p):
                if inside(i, NT):
                    after(pe, S.h_ready, i - 1)
                    after(pe, S.bn_done, i - 1)
                    for k in range(KP):
                        if k % HB == 0:
                            pe.wait_ge(S.x_lo_ready, 2 * i + k // HB + 1)
                        ins = mm3(bk(p)[:, 0:D], (x_hi[p][:, k, :], x_lo[p][:, k, :]),
                                  (wemb_hi[:, k, :], wemb_lo[:, k, :]), k == 0, False)
                        if k == HB - 1:
                            ins.then_inc(S.emb_half, 1)
                    mm(bk(p)[:, 0:D], x_hi[p][:, KP, :], tab[:], False, True).then_inc(S.emb_mm, 1)
                j = i - 2
                if inside(j, NT):
                    pe.wait_ge(S.xhat_ready, j + 1)
                    after(pe, S.xn_lo_ready, j - 1)
                    for k in range(KD):
                        ins = nc.tensor.transpose(bk(2 + p)[:, k * P:(k + 1) * P], xhat[p][:, k * P:(k + 1) * P], ident)
                    ins.then_inc(S.xhat_T, 1)
            pipeline(pe, NT, 2, stage1)

            def project(g, which, pair):
                for m in range(KD):
                    for k in range(KD):
                        ins = mm3(bank[pair][:, m, 0:GC],
                                  (wq_hi[:, which, k, m * P:(m + 1) * P], wq_lo[:, which, k, m * P:(m + 1) * P]),
                                  (xn_hi[:, k, bass.ds(g * GC, GC)], xn_lo[:, k, bass.ds(g * GC, GC)]),
                                  k == 0, k == KD - 1)
                return ins

            def feature(g, pair, hi, lo, sq):
                for m in range(KD):
                    mm3(bank[pair][:, m, 0:GC], (r_hi[:], r_lo[:]), (hi[:, m, :], lo[:, m, :]), True, False)
                    ins = mm(bank[pair][:, m, 0:GC], blk[:], sq[:, m, :], False, True)
                return ins

            def pair_T(g, p, j):
                pe.wait_ge(S.kp_ready, g + 1)
                pe.wait_ge(S.v_ready, g + 1)
                after(pe, S.pair_ready, 4 * g + j - 1)
                if j < 2:
                    pe.wait_ge(S.s_copied, g + 1)
                o = bk(6 + j % 2)
                for c, buf in enumerate((vt[p], kp[p])):
                    for m in range(KD):
                        ins = nc.tensor.transpose(o[:, (2 * c + m) * P:(2 * c + m + 1) * P], buf[:, m, 2 * j:2 * j + 2, :].rearrange("p b t -> p (b t)"),
                                                  ident)
                ins.then_inc(S.pair_T, 1)

            def pair_kv(g, j):
                pe.wait_ge(S.pair_ready, 4 * g + j + 1)
                if j == 2:
                    pe.wait_ge(S.kv_ready, 2 * g + 1)
                for u in range(2):
                    for m in range(KD):
                        ins = mm(bk(4 + u)[:, ((j % 2) * 2 + m) * P:((j % 2) * 2 + m + 1) * P],
                                 kv_t[j % 2][64 * u:64 * u + N, (2 + m) * P:(3 + m) * P],
                                 kv_t[j % 2][64 * u:64 * u + N, m * P:(m + 1) * P], True, True)
                ins.then_inc(S.kv_mm, 1)

            def attend(i, p):
                g, h, ph = i, i - 1, 1 - p
                if inside(h, NG):
                    pe.wait_ge(S.qp_ready, h + 1)
                    after(pe, S.pair_ready, 4 * h)
                    for m in range(KD):
                        ins = mm(bk(6 + m)[:, 0:GC], blk[:], qp[ph][:, m, :], True, True)
                    ins.then_inc(S.s_mm, 1)
                if inside(g, NG):
                    after(pe, S.out_ready, g - 1)
                    project(g, 2, 2).then_inc(S.v_mm, 1)
                if inside(h, NG):
                    pair_T(h, ph, 0)
                    pair_T(h, ph, 1)
                if inside(g, NG):
                    after(pe, S.qp_ready, g)
                    project(g, 0, 0).then_inc(S.q_mm, 1)
                    after(pe, S.kp_ready, g)
                    project(g, 1, 1).then_inc(S.k_mm, 1)
                if inside(h, NG):
                    if inside(g, NG):
                        pe.wait_ge(S.v_ready, g + 1)
                    else:
                        pe.wait_ge(S.out_ready, h)
                    pair_kv(h, 0)
                    pair_kv(h, 1)
                    pair_T(h, ph, 2)
                    pair_T(h, ph, 3)
                if inside(g, NG):
                    pe.wait_ge(S.q_lo_ready, g + 1)
                    feature(g, 0, q_hi, q_lo, s_q).then_inc(S.fq_mm, 1)
                if inside(h, NG):
                    pair_kv(h, 2)
                    pair_kv(h, 3)
                if inside(g, NG):
                    pe.wait_ge(S.k_lo_ready, g + 1)
                    feature(g, 1, k_hi, k_lo, s_k).then_inc(S.fk_mm, 1)
                if inside(h, NG):
                    pe.wait_ge(S.kv_ready, 2 * h + 2)
                    for b in range(GI):
                        for m in range(KD):
                            c = (b // 2 % 2) * 2 * P + m * P
                            ins = mm(bk(4 + m)[:, b * N:(b + 1) * N], kv_sb[:, b // 4, b % 2, c:c + P],
                                     qp[ph][:, m, b * N:(b + 1) * N], True, True)
                    ins.then_inc(S.o_mm, 1)
            pe.wait_ge(S.w_split, 1)
            pe.wait_ge(S.blk_done, 1)
            pe.wait_ge(S.xn_lo_ready, NT)
            pipeline(pe, NG, 1, attend, 2)

            def wo(i, p):
                after(pe, S.h2_kept, i - 3)
                o = bk(p)[:, 0:D]
                mm(o, ident, h_tok[:, bass.ds(i, 1), :].rearrange("p a d -> p (a d)"), True, False)
                mm(o, ones_r[:], bo_split[:], False, False)
                pe.wait_ge(S.ol_ready, i + 1)
                for m in range(KD):
                    ins = mm3(o, (oh[p][:, m, :], ol[p][:, m, :]), (wo_hi[:, m, :], wo_lo[:, m, :]),
                              False, m == KD - 1)
                ins.then_inc(S.wo_mm, 1)
            pe.wait_ge(S.bo_ready, 1)
            pipeline(pe, NT, 0, wo, by=4)

            def gate_tile(i, p):
                if inside(i, NT):
                    pe.wait_ge(S.g_ready, i + 1)
                    after(pe, S.gT_ready, i - 1)
                    for k in range(KD):
                        ins = nc.tensor.transpose(bk(2 + p % 2)[:, k * P:(k + 1) * P], g_tok[p][:, k * P:(k + 1) * P], ident)
                    ins.then_inc(S.gT_mm, 1)
                j = i - 1
                if inside(j, NT):
                    pe.wait_ge(S.gT_ready, j + 1)
                    for k in range(KD):
                        ins = mm(bk(4)[:, bass.ds(j * NE, NE)], gT[(p + 1) % 2][:, k, :], gate_sb[:, k, :], k == 0, k == KD - 1)
                    ins.then_inc(S.logits_mm, 1)
            pe.wait_ge(S.out_ready, NG)
            pipeline(pe, NT, 1, gate_tile, by=4)

            pe.wait_ge(S.rt, 8)
            mm(bk(5)[:, 0:R], upper, onehot[:].rearrange("p e i -> p (e i)"), True, True)
            mm(bk(6)[:, 0:R], ones, onehot[:].rearrange("p e i -> p (e i)"), True, True).then_inc(S.rt_pe, 1)
            pe.wait_ge(S.payload_ready, 3)

            def table(i, p):
                pe.wait_ge(S.hot_ready, i + 1)
                first = isinstance(i, int) and i == 0
                last = isinstance(i, int) and i == NT - 1
                mm(bk(7)[:, 0:3 * NS], sp_hot[p][:], payload[:, bass.ds(i, 1), :, :].rearrange("p a c s -> p (a c s)"),
                   first, last).then_inc(S.hot_mm, 1)
            pipeline(pe, NT, 0, table)

            def x_T(t, p):
                pe.wait_ge(row_in[p], 16 * (t // 2 + 1))
                after(pe, S.xT_ready, t)
                for k in range(KD):
                    ins = nc.tensor.transpose(bk(6)[:, k * P:(k + 1) * P], row[p][:, k * P:(k + 1) * P], ident)
                ins.then_inc(S.x_T, 1)

            def weights(e, start, n):
                return wff[:, bass.ds(e, 1), start:start + n].rearrange("p a n -> p (a n)")

            def body4(i, p):
                if inside(i, NS):
                    x_T(i, p)
                t = i - 2
                if inside(t, NS):
                    pe.wait_ge(S.act_ready, t + 1)
                    after(pe, S.actT_a, t)
                    after(pe, S.actT_b, t)
                    for k in range(KF):
                        ins = nc.tensor.transpose(bk(4 + k // 4)[:, (k % 4) * P:(k % 4 + 1) * P],
                                                  act_f[p][:, k * P:(k + 1) * P], ident)
                    ins.then_inc(S.act_T, 1)
                t = i - 1
                if inside(t, NS):
                    e = pe.value_load(e_tile[0:1, bass.ds(t, 1)], min_val=0, max_val=NE - 1)
                    pe.wait_ge(S.xT_ready, t + 1)
                    after(pe, S.pre_act, t - 1)
                    for f in range(2):
                        for k in range(KD):
                            ins = mm(bank[1 - p][:, f, :], xT[1 - p][:, k, :], weights(e, k * FF + f * 512, 512),
                                     k == 0, k == KD - 1)
                    ins.then_inc(S.s1_mm, 1)
                t = i - 2
                if inside(t, NS):
                    e = pe.value_load(e_tile[0:1, bass.ds(t, 1)], min_val=0, max_val=NE - 1)
                    after(pe, S.o_ready, t)
                    pe.wait_ge(S.actT_a, t + 1)
                    for k in range(KF):
                        if k == KF // 2:
                            pe.wait_ge(S.actT_b, t + 1)
                        ins = mm(bk(7)[:, 0:D], actT[p][:, k, :], weights(e, KD * FF + k * D, D), k == 0, k == KF - 1)
                    ins.then_inc(S.s2_mm, 1)
            pe.wait_ge(S.tables, 1)
            pe.wait_ge(S.wff_in, 16 * 2 * NE)
            pipeline(pe, NS, 2, body4)


def kernel(**inputs):
    import numpy as np
    import concourse.bacc as bacc
    from concourse.bass_utils import run_bass_kernel_spmd

    f = np.float32

    def blocks(w):
        k, m = w.shape
        return np.ascontiguousarray(w.reshape(k // P, P, m).transpose(1, 0, 2).reshape(P, -1))

    x = np.asarray(inputs["x"])
    patches = np.zeros((PIX, IMGS, N), x.dtype)
    patches[:, :, 1:] = x.reshape(IMGS, 3, 6, 16, 6, 16).transpose(1, 3, 5, 0, 2, 4).reshape(PIX, IMGS, N - 1)
    xin = np.zeros((NT, P, KP + 1, P), x.dtype)
    cols = np.zeros((PIX, NT * P), x.dtype)
    cols[:, :T] = patches.reshape(PIX, T)
    xin[:, :, :KP, :] = cols.reshape(KP, P, NT, P).transpose(2, 1, 0, 3)
    tok = np.arange(NT * P) % N
    sel = np.zeros((P, NT * P), f)
    sel[tok, np.arange(NT * P)] = 1
    sel[64 + tok, np.arange(NT * P)] = 1
    xin[:, :, KP, :] = sel.reshape(P, NT, P).transpose(1, 0, 2)

    w_all = np.concatenate([blocks(np.asarray(inputs[n]).T) for n in
                            ("L0_tok_W", "L0_attn_Wq", "L0_attn_Wk", "L0_attn_Wv", "L0_attn_Wo")], axis=1)
    head = np.arange(P) // HD
    consts = np.concatenate([
        np.eye(P, dtype=f), (head[:, None] == head[None, :]).astype(f),
        (np.arange(P)[:, None] < np.arange(P)[None, :]).astype(f), np.ones((P, P), f),
        np.tile(np.arange(P, dtype=f), (P, 1)),
        np.tile((np.arange(P) < T - (NT - 1) * P).astype(f)[:, None], (1, 2))], axis=1)
    number = np.arange(NT * P).reshape(NT, P).T
    ids = np.where(number < T, number + 1, 0).astype(f)
    small = np.concatenate([np.asarray(inputs[n]).reshape(KD, P).T for n in
                            ("L0_attn_bq", "L0_attn_bk", "L0_attn_bv", "L0_ffn_rms_w")]
                           + [blocks(np.asarray(inputs["L0_ffn_gate_w"]).T)], axis=1)
    arrays = {
        "xin": xin, "w_all": w_all, "Rm": inputs["L0_attn_R"], "tok_b": inputs["L0_tok_b"],
        "cls_tok": inputs["L0_tok_class_token"], "pos": inputs["L0_tok_pos_embedding"],
        "small": small, "bo": inputs["L0_attn_bo"],
        "W1": inputs["L0_ffn_W1"], "b1": inputs["L0_ffn_b1"], "W2": inputs["L0_ffn_W2"], "b2": inputs["L0_ffn_b2"],
        "consts": consts, "ids": ids,
    }
    arrays = {k: np.ascontiguousarray(v) for k, v in arrays.items()}
    nc = bacc.Bacc("TRN2", target_bir_lowering=False, num_devices=1)
    args = [nc.dram_tensor(k, v.shape, mybir.dt.from_np(v.dtype), kind="ExternalInput").ap() for k, v in arrays.items()]
    out = nc.dram_tensor("out", (IMGS, N, D), F32, kind="ExternalOutput").ap()
    vit_kernel(nc, *args, out)
    r = run_bass_kernel_spmd(nc, [arrays], core_ids=[0])
    return r.results[0]["out"]
```

```python
from contextlib import ExitStack

import concourse.bass as bass
from concourse import mybir

F32 = mybir.dt.float32
F32R = mybir.dt.float32r
I32 = mybir.dt.int32
ALU = mybir.AluOpType
ACT = mybir.ActivationFunctionType
AX = mybir.AxisListType

P = 128
IMGS, N = 64, 37
T = IMGS * N
NT = -(-T // P)
D = 256
KD = D // P
PIX = 768
KP = PIX // P
HD = 16
GI = 8
NG = IMGS // GI
GC = GI * N
SL = 64
NE, FF = 8, 1024
KF = FF // P
KS = 5
NS = (T + NE * (P - 1)) // P
LN_EPS, RMS_EPS, Z_EPS = 1e-5, 1e-6, 1e-8
KB = 1024


def pipeline(eng, n, skew, body, first=None, by=2, start=0):
    lo = first or (skew + 1 + by) // by * by
    hi = n // by * by
    for i in range(start, lo):
        body(i, i % by)
    with eng.Fori(lo // by, hi // by) as j:
        for u in range(by):
            body(by * j + u, u)
    for i in range(hi, n + skew):
        body(i, i % by)


def inside(i, n):
    return not isinstance(i, int) or 0 <= i < n


def after(eng, sem, count):
    if not isinstance(count, int) or count > 0:
        eng.wait_ge(sem, count)


def settle(eng, sem, count, settled, value):
    if not isinstance(count, int):
        eng.wait_ge(settled, value)
    eng.wait_ge(sem, count)


def vit_kernel(nc, xin, w_all, Rm, tok_b, cls_tok, pos, small_d, bo, W1, b1, W2, b2, consts, ids, out):
    with ExitStack() as ctx:
        def at(name, shape, dt, offset):
            return nc.alloc_sbuf_tensor_at(name, shape, dt, offset=offset)

        def sem(name):
            return ctx.enter_context(nc.semaphore(name))

        arena_bytes = 212832
        base = -(-nc.sbuf_base // 32) * 32
        ctx.enter_context(nc.sbuf_tensor("arena", [P, arena_bytes // 4], F32))

        class Region:
            def __init__(self, start, end):
                self.at, self.end = start, end

            def put(self, name, shape, dt):
                size = 4
                for s in shape[1:]:
                    size *= s
                size = -(-size // 32) * 32
                t = at(name, shape, dt, base + self.at)
                self.at += size
                assert self.at <= self.end, (name, self.at, self.end)
                return t

        EB = 4 * (KD * FF + KF * D)
        wff = at("wff", [P, NE, KD * FF + KF * D], F32, base)
        WEMB = KP * D
        WQKV = 3 * KD * D
        top0 = NE * EB

        low = Region(0, 2 * EB)
        wemb_hi = low.put("wemb_hi", [P, KP, D], F32R)
        wemb_lo = low.put("wemb_lo", [P, KP, D], F32R)
        x_raw = [low.put(f"x_raw{p}", [P, KP + 1, P], F32) for p in range(2)]
        x_hi = [low.put(f"x_hi{p}", [P, KP + 1, P], F32R) for p in range(2)]
        xhat = [low.put(f"xhat{p}", [P, D], F32) for p in range(2)]
        mid = Region(2 * EB, 5 * EB)
        xn_hi = mid.put("xn_hi", [P, KD, NT * P], F32R)
        xn_lo = mid.put("xn_lo", [P, KD, NT * P], F32R)
        vt1 = mid.put("vt1", [P, KD, GI, SL], F32)
        s_sb = mid.put("s_sb", [P, KD, GC], F32)
        late1 = Region(6 * EB, top0)
        w_raw = late1.put("w_raw", [P, WEMB + WQKV + KD * D], F32)
        x_lo = [late1.put(f"x_lo{p}", [P, KP, P], F32R) for p in range(2)]
        x_raw += [late1.put(f"x_raw{p}", [P, KP + 1, P], F32) for p in range(2, 4)]
        tab_raw = late1.put("tab_raw", [P, D], F32)
        tab_add = late1.put("tab_add", [P, D], F32)
        tab = late1.put("tab", [P, D], F32R)
        tab_tmp = late1.put("tab_tmp", [P, D], F32R)
        late2 = Region(6 * EB, top0)
        outT = late2.put("outT", [P, KD, NT * P], F32)
        kv_sb = late2.put("kv_sb", [P, 2, 2, 4 * P], F32)
        vt = [late2.put("vt0", [P, KD, GI, SL], F32), vt1]
        top = Region(top0, arena_bytes)
        cst = top.put("cst", [P, 5 * P + 2], F32)
        ident, mask = cst[:, 0:P], cst[:, P:2 * P]
        upper, ones = cst[:, 2 * P:3 * P], cst[:, 3 * P:4 * P]
        iota = cst[:, 4 * P:5 * P]
        valid = cst[:, 5 * P:5 * P + 1]
        id1 = top.put("id1", [P, NT], F32)
        small = top.put("small", [P, (3 + 1 + NE) * KD], F32)
        b_c = small[:, 0:3 * KD].rearrange("p (a k) -> p a k", k=KD)
        rms_c = small[:, 3 * KD:4 * KD]
        gate_sb = small[:, 4 * KD:].rearrange("p (k e) -> p k e", k=KD)
        b1_c = top.put("b1_c", [P, NE, KF], F32)
        eps_ln = top.put("eps_ln", [P, 1], F32)
        eps_n = top.put("eps_n", [P, 1], F32)
        eps_z = top.put("eps_z", [P, 1], F32)
        gate_rms = top.put("gate_rms", [P, KD, NE], F32)
        upper_r = top.put("upper_r", [P, P], F32R)
        unit = top.put("unit", [P, NE * NT], F32)
        mr = top.put("mr", [P, NT, 2], F32)
        std = top.put("std", [P, 2], F32)
        rstd = top.put("rstd", [P, 2], F32)
        mvt = [top.put(f"mvt{p}", [P, 2], F32) for p in range(2)]
        bn = [top.put(f"bn{p}", [P, 6], F32) for p in range(2)]
        gidx = top.put("gidx", [P, NS], I32)
        sidx = top.put("sidx", [P, NS], I32)
        slot_score = top.put("slot_score", [P, NS], F32)
        gi = [top.put(f"gi{p}", [P, 1], I32) for p in range(2)]
        si = [top.put(f"si{p}", [P, 1], I32) for p in range(2)]
        spare = top.put("spare", [P, 1], F32)
        e_tile = top.put("e_tile", [P, NS], I32)
        t19_0 = top.put("t19_0", [P, NT], F32)
        t19_1 = top.put("t19_1", [P, NT], F32)
        t19_2 = top.put("t19_2", [P, NT], F32)
        h_start = top.at
        h_tok = top.put("h_tok", [P, NT, D], F32)
        bias_start = top.at
        w1_s = [top.put(f"w1_s{p}", [P, KD, FF], F32) for p in range(2)]
        w2_hi = [top.put(f"w2_hi{p}", [P, KS, D], F32R) for p in range(2)]
        w2_lo = [top.put(f"w2_lo{p}", [P, KS, D], F32R) for p in range(2)]
        b2_bc = top.put("b2_bc", [P, NE, D], F32)
        work_start = top.at
        ph2 = Region(bias_start, work_start)
        wq_hi = ph2.put("wq_hi", [P, 3, KD, D], F32R)
        wq_lo = ph2.put("wq_lo", [P, 3, KD, D], F32R)
        blk = ph2.put("blk", [P, P], F32)
        r_hi = ph2.put("r_hi", [P, P], F32R)
        r_lo = ph2.put("r_lo", [P, P], F32R)
        q_hi = ph2.put("q_hi", [P, KD, GC], F32R)
        q_lo = ph2.put("q_lo", [P, KD, GC], F32R)
        k_hi = ph2.put("k_hi", [P, KD, GC], F32R)
        k_lo = ph2.put("k_lo", [P, KD, GC], F32R)
        kp = [ph2.put(f"kp{p}", [P, KD, GI, SL], F32) for p in range(2)]
        s_q = ph2.put("s_q", [P, KD, GC], F32)
        work = Region(work_start, arena_bytes)
        wo_hi = work.put("wo_hi", [P, KD, D], F32R)
        wo_lo = work.put("wo_lo", [P, KD, D], F32R)
        bo_split = work.put("bo_split", [P, D], F32R)
        ones_r = work.put("ones_r", [P, P], F32R)
        work2 = Region(work.at, arena_bytes)
        rbd_raw = ph2.put("rbd_raw", [P, P], F32)
        bo_raw = ph2.put("bo_raw", [P, D], F32)
        bo_tmp = ph2.put("bo_tmp", [P, D], F32R)
        kv_t = [(work2 if r else ph2).put(f"kv_t{r}", [P, 4 * P], F32) for r in range(2)]
        qp = [work2.put("qp0", [P, KD, GC], F32), mid.put("qp1", [P, KD, GC], F32)]
        s_k = ph2.put("s_k", [P, KD, GC], F32)
        work3 = Region(work.at, arena_bytes)
        oh = [(ph2 if p < 2 else work3).put(f"oh{p}", [P, KD, P], F32R) for p in range(4)]
        ol = [(ph2 if p < 2 else work3).put(f"ol{p}", [P, KD, P], F32R) for p in range(4)]
        late3 = Region(6 * EB + 4 * KD * NT * P, top0)
        g_tok = [late3.put(f"g_tok{p}", [P, D], F32) for p in range(2)]
        gT = [late3.put(f"gT{p}", [P, KD, P], F32) for p in range(2)]
        R = NE * NT
        rw = Region(work_start, arena_bytes)
        sp_hot = rw.put("sp_hot", [P, NT, P], F32R)
        rr = Region(h_start, bias_start)
        rq = Region(bias_start, work_start)
        first_max = rq.put("first_max", [P, NE, NT], F32)
        onehot = rw.put("onehot", [P, NE, NT], F32R)
        rt1 = rq.put("rt1", [P, NE, NT], F32)
        rt2 = rq.put("rt2", [P, NE, NT], F32)
        tot = rq.put("tot", [P, NE, NT], F32)
        mx = rw.put("mx", [P, NT], F32)
        t19 = [t19_0, t19_1, t19_2] + [rw.put(f"t19_{i}", [P, NT], F32) for i in range(3, 6)]
        slot_i = rw.put("slot_i", [P, NT], I32)
        st_i = rw.put("st_i", [P, NT], I32)
        sp_i = rw.put("sp_i", [P, NT], I32)
        t8 = [rq.put(f"t8_{i}", [P, NE], F32) for i in range(6)]
        t8i = rq.put("t8i", [P, NE], I32)
        t26 = [rq.put(f"t26_{i}", [P, NS], F32) for i in range(3)]
        cmp26 = rq.put("cmp26", [P, NS, NE], F32)
        st_hot = rr.put("st_hot", [P, NT, NS], F32)
        sc_hi = rw.put("sc_hi", [P, NT], F32R)
        payload = rr.put("payload", [P, NT, 3, NS], F32R)
        ffn_a, ffn_b = Region(h_start, bias_start), Region(work_start, arena_bytes)
        act_f = [ffn_a.put(f"act_f{p}", [P, KF, P], F32) for p in range(2)]
        act_hi = [ffn_a.put(f"act_hi{p}", [P, KS, P], F32R) for p in range(2)]
        act_lo = [ffn_b.put(f"act_lo{p}", [P, KS, P], F32R) for p in range(2)]
        xT = [ffn_b.put(f"xT{p}", [P, KD, P], F32) for p in range(2)]
        row = [ffn_b.put(f"row{p}", [P, D + 2], F32) for p in range(2)]
        h2c = [ffn_b.put(f"h2c{p}", [P, D], F32) for p in range(2)]
        x_sb = ffn_a.put("x_sb", [P, D], F32)
        o_sb = ffn_a.put("o_sb", [P, D], F32)

        bank = [ctx.enter_context(nc.psum_tensor(f"bank{i}", [P, 2, 512], F32)) for i in range(4)]

        def bk(i):
            return bank[i // 2][:, i % 2, :]

        rows_d = nc.dram_tensor("rows_scratch", [NT * P, D + 2], F32).ap()
        out_rows = out.rearrange("b n d -> (b n) d")

        s = {}
        for name in (
            "w_in0 w_in1 w_rest_in tab_in cst_in zeroed w_emb_hi w_emb_lo w_hi w_split tab_sum tab_hi tab_done blk_done rbd_zero r_in "
            "x_in0 x_in1 x_in2 x_in3 x_hi_ready x_lo_ready emb_half emb_mm h_ready bn_done var_ready std_ready rstd_ready xhat_ready "
            "xhat_T xn_hi_ready xn_lo_ready tail_zero bo_hi bo_ready "
            "v_mm q_mm k_mm v_ready q_hi_ready q_lo_ready sq_ready k_hi_ready k_lo_ready sk_ready fq_mm fk_mm "
            "qp_ready kp_ready pair_T pair_ready kv_mm kv_ready z_ready s_mm o_mm s_copied out_ready "
            "oh_ready ol_ready wo_mm h2_bn h2_mv h2_std h2_rstd h2_kept mr_saved g_ready h2_saved gate_done gT_mm gT_ready logits_mm "
            "rt rt_act rt_pe st_hot_ready hot_ready hot_mm payload_ready payload_pool gather_table tables "
            "wff_in bias_in "
            "gi_ready si_ready row_in0 row_in1 x_ready row_copied x_T xT_ready w1_a w1_b w2_hi_ready w2_lo_ready s1_mm pre_act act_ready act_hi_ready act_lo_ready s2_mm b2_added o_ready "
            "o_saved"
        ).split():
            s[name] = sem(name)
        S = type("S", (), s)
        x_in = [S.x_in0, S.x_in1, S.x_in2, S.x_in3]
        row_in = [S.row_in0, S.row_in1]

        block = ctx.enter_context(nc.Block())
        PIECES = {NT - 3: 2, NT - 2: 0, NT - 1: 1, NT: 3}

        def piece(wq, wo, c):
            return wq[:, c, :, :].rearrange("p k d -> p (k d)") if c < 3 else wo[:].rearrange("p k d -> p (k d)")

        CST = 16 * 6
        WO_BANK = (0, 1, 5, 6)
        W2S = KD * FF + (KF - KS) * D
        HB = KP // 2

        @block.sync
        def _(sp):
            def load_x(i, p):
                after(sp, S.x_lo_ready, 2 * (i - 3))
                sp.dma_start(x_raw[p][:], xin[bass.ds(i, 1)].rearrange("a p k t -> (a p) k t")
                             if not isinstance(i, int) else xin[i]).then_inc(x_in[p], 16)

            wh = HB * D
            sp.dma_start(w_raw[:, 0:wh], w_all[:, 0:wh]).then_inc(S.w_in0, 16)
            load_x(0, 0)
            sp.dma_start(w_raw[:, wh:WEMB], w_all[:, wh:WEMB]).then_inc(S.w_in1, 16)
            for o in (0, 64):
                sp.dma_start(tab_raw[o:o + N, :], pos[0]).then_inc(S.tab_in, 16)
                sp.dma_start(tab_add[o:o + 1, :], cls_tok[0]).then_inc(S.tab_in, 16)
                sp.dma_start(tab_add[o + 1:o + N, :], tok_b[None, :].broadcast_to([N - 1, D])).then_inc(S.tab_in, 16)
            load_x(1, 1)
            load_x(2, 2)
            sp.dma_start(cst[:], consts).then_inc(S.cst_in, 16)
            load_x(3, 3)
            sp.dma_start(small[:], small_d).then_inc(S.cst_in, 16)
            sp.dma_start(id1[:], ids).then_inc(S.cst_in, 16)
            sp.dma_start(b1_c[:], b1).then_inc(S.cst_in, 16)
            for o in (0, 64):
                sp.dma_start(bo_raw[o:o + 1, :], bo[None, :]).then_inc(S.cst_in, 16)
            sp.dma_start(w_raw[:, WEMB:], w_all[:, WEMB:]).then_inc(S.w_rest_in, 16)
            sp.wait_ge(S.rbd_zero, 1)
            for h in range(P // HD):
                sp.dma_start(rbd_raw[h * HD:(h + 1) * HD, h * HD:(h + 1) * HD], Rm).then_inc(S.r_in, 16)
            with sp.Fori(1, NT // 4) as j:
                for p in range(4):
                    load_x(4 * j + p, p)
            for i in range(NT // 4 * 4, NT):
                load_x(i, i % 4)

            def load_expert(e, done):
                sp.dma_start(wff[:, e, 0:KD * FF].rearrange("p (k f) -> p k f", k=KD),
                             W1[e].rearrange("(k p) f -> p k f", p=P)).then_inc(done, 16)
                sp.dma_start(wff[:, e, KD * FF:].rearrange("p (k d) -> p k d", k=KF),
                             W2[e].rearrange("(k p) d -> p k d", p=P)).then_inc(done, 16)

            sp.wait_ge(S.xn_lo_ready, NT)
            load_expert(0, S.wff_in)
            load_expert(1, S.wff_in)
            load_expert(5, S.wff_in)
            sp.wait_ge(S.out_ready, NG)
            for e in range(2, 5):
                load_expert(e, S.wff_in)
            for c in range(5):
                i, n = 4 * c, min(4, NT - 4 * c)
                sp.wait_ge(S.h2_kept, i + n)
                sp.dma_start(rows_d[i * P:(i + n) * P, 0:D].rearrange("(i p) d -> p i d", p=P),
                             h_tok[:, i:i + n, :]).then_inc(S.h2_saved, 16)
            sp.wait_ge(S.g_ready, NT)
            sp.dma_start(rows_d[:, D:].rearrange("(i p) d -> p i d", p=P), mr[:]).then_inc(S.mr_saved, 16)
            sp.dma_start(b2_bc[:], b2[None].broadcast_to([P, NE, D])).then_inc(S.bias_in, 16)
            sp.wait_ge(S.logits_mm, NT)
            for e in range(6, NE):
                load_expert(e, S.wff_in)

        @block.gpsimd
        def _(pool):
            nc.gpsimd.memset(rbd_raw[:], 0.0).then_inc(S.rbd_zero, 1)
            for p in range(2):
                nc.gpsimd.memset(kp[p][:, :, :, N:], 0.0).then_inc(S.zeroed, 1)
            nc.gpsimd.memset(vt[1][:, :, :, N:], 0.0).then_inc(S.zeroed, 1)
            nc.gpsimd.memset(eps_ln[:], LN_EPS).then_inc(S.zeroed, 1)
            nc.gpsimd.memset(eps_n[:], RMS_EPS * LN_EPS)
            nc.gpsimd.memset(spare[:], 0.0)
            nc.gpsimd.memset(unit[:], 1.0)
            nc.gpsimd.memset(eps_z[:], Z_EPS).then_inc(S.zeroed, 1)
            def body(i, p):
                for h in range(2):
                    settle(pool, S.x_hi_ready, 2 * i + h + 1, S.cst_in, CST)
                    after(pool, S.emb_mm if h else S.emb_half, i - 1)
                    ks = slice(h * HB, h * HB + HB)
                    nc.gpsimd.tensor_tensor(x_lo[p % 2][:, ks, :], x_raw[p][:, ks, :], x_hi[p % 2][:, ks, :].bitcast(F32),
                                            ALU.subtract).then_inc(S.x_lo_ready, 1)
            pipeline(pool, NT, 0, body, by=4)
            pool.wait_ge(S.xn_lo_ready, NT)
            nc.gpsimd.memset(vt[0][:, :, :, N:], 0.0).then_inc(S.tail_zero, 1)
            nc.gpsimd.memset(outT[:, :, T:], 0.0).then_inc(S.tail_zero, 1)

            def low_out(i, p):
                settle(pool, S.oh_ready, i + 1, S.cst_in, CST)
                after(pool, S.wo_mm, i - 3)
                nc.gpsimd.tensor_tensor(ol[p][:], outT[:, :, bass.ds(i * P, P)], oh[p][:].bitcast(F32),
                                        ALU.subtract).then_inc(S.ol_ready, 1)
            pipeline(pool, NT, 0, low_out, by=4)

            pool.wait_ge(S.st_hot_ready, 1)
            for c, val in ((0, id1[:]), (2, t19_2[:])):
                nc.gpsimd.tensor_tensor(payload[:, :, c, :], st_hot[:], val[:, :, None].broadcast_to([P, NT, NS]),
                                        ALU.mult).then_inc(S.payload_pool, 1)

            pool.wait_ge(S.h2_saved, 16 * 5)
            pool.wait_ge(S.mr_saved, 16)

            def gather(t, p):
                pool.wait_ge(S.gather_table, 1)
                after(pool, S.x_ready, t - 1)
                after(pool, S.row_copied, t - 1)
                after(pool, row_in[p], 16 * (t // 2))
                nc.gpsimd.tensor_copy(gi[p][:], gidx[:, bass.ds(t, 1)]).then_inc(S.gi_ready, 1)
                pool.wait_ge(S.gi_ready, t + 1)
                nc.gpsimd.tensor_tensor(spare[:], spare[:], spare[:], ALU.add)
                nc.gpsimd.indirect_dma_start(
                    row[p][:], None, rows_d, bass.IndirectOffsetOnAxis(ap=gi[p][:, 0:1], axis=0)
                ).then_inc(row_in[p], 16)

            def scatter(t, p):
                if isinstance(t, int):
                    pool.wait_ge(S.tables, 1)
                settle(pool, S.o_ready, t + 1, S.tables, 1)
                after(pool, S.o_saved, 16 * t)
                nc.gpsimd.tensor_copy(si[p][:], sidx[:, bass.ds(t, 1)]).then_inc(S.si_ready, 1)
                pool.wait_ge(S.si_ready, t + 1)
                nc.gpsimd.tensor_tensor(spare[:], spare[:], spare[:], ALU.add)
                nc.gpsimd.indirect_dma_start(
                    out_rows, bass.IndirectOffsetOnAxis(ap=si[p][:, 0:1], axis=0), o_sb[:], None,
                    bounds_check=T - 1, oob_is_err=False).then_inc(S.o_saved, 16)

            def body4(t, p):
                if inside(t, NS):
                    gather(t, p)
                if inside(t - 2, NS):
                    settle(pool, S.act_hi_ready, t - 2 + 1, S.gather_table, 1)
                    after(pool, S.s2_mm, t - 2 - 1)
                    nc.gpsimd.tensor_tensor(act_lo[p][:], act_f[p][:, KF - KS:, :], act_hi[p][:].bitcast(F32),
                                            ALU.subtract).then_inc(S.act_lo_ready, 1)
                if inside(t - 3, NS):
                    scatter(t - 3, 1 - p)
            pipeline(pool, NS, 3, body4)
            pool.wait_ge(S.o_saved, 16 * NS)

        @block.scalar
        def _(act):
            def w_half(h):
                act.wait_ge(S.w_in1 if h else S.w_in0, 16)
                nc.scalar.copy(wemb_hi[:, h * HB:(h + 1) * HB, :].rearrange("p k d -> p (k d)"),
                               w_raw[:, h * HB * D:(h + 1) * HB * D]).then_inc(S.w_emb_hi, 1)
            w_half(0)

            def body(i, p):
                if inside(i, NT):
                    act.wait_ge(x_in[p], 16 * (i // 4 + 1))
                    for h in range(2):
                        after(act, S.emb_mm if h else S.emb_half, i - 1)
                        ks = slice(HB, KP + 1) if h else slice(0, HB)
                        nc.scalar.copy(x_hi[p % 2][:, ks, :], x_raw[p][:, ks, :]).then_inc(S.x_hi_ready, 1)
                    if isinstance(i, int) and i == 0:
                        w_half(1)
                    if isinstance(i, int) and i == 1:
                        act.wait_ge(S.zeroed, 5)
                j = i - 2
                if inside(j, NT):
                    act.wait_ge(S.var_ready, j + 1)
                    nc.scalar.activation(std[:, p % 2:p % 2 + 1], mvt[p % 2][:, 1:2], ACT.Sqrt,
                                         bias=eps_ln[:, 0:1]).then_inc(S.std_ready, 1)
                j = i - 3
                if inside(j, NT):
                    act.wait_ge(S.xhat_T, j + 1)
                    nc.scalar.copy(xn_hi[:, :, bass.ds(j * P, P)],
                                   bk(3 - p % 2)[:, 0:D].rearrange("p (k t) -> p k t", k=KD)).then_inc(S.xn_hi_ready, 1)
                if isinstance(i, int) and i in PIECES:
                    act.wait_ge(S.w_rest_in, 16)
                    c = PIECES[i]
                    nc.scalar.copy(piece(wq_hi, wo_hi, c), w_raw[:, WEMB + c * KD * D:WEMB + (c + 1) * KD * D]).then_inc(S.w_hi, 1)
                    if c == 3:
                        act.wait_ge(S.r_in, 16 * (P // HD))
                        nc.scalar.mul(r_hi[:], rbd_raw[:], 0.25).then_inc(S.w_hi, 1)
            pipeline(act, NT, 3, body, 4, 4)

            def proj(g, mm, pair, hi, hi_ready, sq, sq_ready, bias_row, free):
                act.wait_ge(mm, g + 1)
                after(act, free, g)
                for m in range(KD):
                    ins = nc.scalar.activation(hi[:, m, :], bank[pair][:, m, 0:GC], ACT.Identity,
                                               bias=b_c[:, bias_row, m:m + 1])
                ins.then_inc(hi_ready, 1)
                for m in range(KD):
                    ins = nc.scalar.activation(sq[:, m, :], bank[pair][:, m, 0:GC], ACT.Square,
                                               bias=b_c[:, bias_row, m:m + 1])
                ins.then_inc(sq_ready, 1)

            def pairs(g, js):
                for j in js:
                    act.wait_ge(S.pair_T, 4 * g + j + 1)
                    after(act, S.kv_mm, 4 * g + j - 1)
                    nc.scalar.copy(kv_t[j % 2][:], bk(6 + j % 2)).then_inc(S.pair_ready, 1)

            def residual(i, p):
                q = p % 2
                if inside(i, NT):
                    after(act, S.wo_mm, i - 3)
                    nc.scalar.copy(oh[p][:], outT[:, :, bass.ds(i * P, P)]).then_inc(S.oh_ready, 1)
                j = i - 2
                if inside(j, NT):
                    act.wait_ge(S.h2_bn, j + 1)
                    nc.scalar.copy(h_tok[:, bass.ds(j, 1), :].rearrange("p a d -> p (a d)"),
                                   bk(WO_BANK[(p + 2) % 4])[:, 0:D]).then_inc(S.h2_kept, 1)
                    act.wait_ge(S.h2_mv, j + 1)
                    nc.scalar.activation(std[:, q:q + 1], mvt[q][:, 1:2], ACT.Sqrt, bias=eps_n[:, 0:1],
                                         scale=1.0 + RMS_EPS).then_inc(S.h2_std, 1)
                j = i - 3
                if inside(j, NT):
                    act.wait_ge(S.gT_mm, j + 1)
                    nc.scalar.copy(gT[1 - q][:].rearrange("p k t -> p (k t)"), bk(3 - q)[:, 0:D]).then_inc(S.gT_ready, 1)
            def attend(i, p):
                g, h = i, i - 1
                if isinstance(i, int) and i == NG:
                    act.wait_ge(S.out_ready, 2)
                    residual(0, 0)
                    residual(1, 1)
                if inside(h, NG):
                    act.wait_ge(S.s_mm, h + 1)
                    after(act, S.out_ready, h)
                    nc.scalar.activation(s_sb[:], bank[2][:, :, 0:GC], ACT.Identity, bias=eps_z[:, 0:1],
                                         scale=-2.0 * HD).then_inc(S.s_copied, 1)
                if inside(g, NG):
                    proj(g, S.q_mm, 0, q_hi, S.q_hi_ready, s_q, S.sq_ready, 0, S.fq_mm)
                if inside(h, NG):
                    pairs(h, (0, 1))
                if inside(g, NG):
                    proj(g, S.k_mm, 1, k_hi, S.k_hi_ready, s_k, S.sk_ready, 1, S.fk_mm)
                if inside(h, NG):
                    pairs(h, (2, 3))
                if inside(g, NG):
                    act.wait_ge(S.fq_mm, g + 1)
                    after(act, S.o_mm, g - 1)
                    nc.scalar.activation(qp[p][:], bank[0][:, :, 0:GC], ACT.Exp).then_inc(S.qp_ready, 1)
                    act.wait_ge(S.fk_mm, g + 1)
                    after(act, S.kv_mm, 4 * (g - 1))
                    nc.scalar.activation(kp[p][:, :, :, 0:N], bank[1][:, :, 0:GC].rearrange("p m (b t) -> p m b t", b=GI),
                                         ACT.Exp).then_inc(S.kp_ready, 1)
            pipeline(act, NG, 1, attend, 2)

            act.wait_ge(S.kv_mm, 4 * NG)
            act.wait_ge(S.tail_zero, 2)
            residual(2, 2)
            act.wait_ge(S.out_ready, NG)
            pipeline(act, NT, 3, residual, 4, 4, start=3)
            act.wait_ge(S.rt, 3)
            nc.scalar.activation(rt2[:], rt1[:], ACT.Exp).then_inc(S.rt_act, 1)

            def body4(i, p):
                q = 1 - p
                t = i - 2
                if inside(t, NS):
                    e = act.value_load(e_tile[0:1, bass.ds(t, 1)], min_val=0, max_val=NE - 1)
                    after(act, S.s2_mm, t - 1)
                    nc.scalar.copy(w2_hi[p][:].rearrange("p k d -> p (k d)"),
                                   wff[:, bass.ds(e, 1), W2S:].rearrange("p a n -> p (a n)")).then_inc(S.w2_hi_ready, 1)
                t = i - 1
                if inside(t, NS):
                    e = act.value_load(e_tile[0:1, bass.ds(t, 1)], min_val=0, max_val=NE - 1)
                    after(act, S.s1_mm, t - 1)
                    nc.scalar.copy(w1_s[q][:, 0, :], wff[:, bass.ds(e, 1), 0:FF].rearrange("p a n -> p (a n)")).then_inc(S.w1_a, 1)

                def silu(t):
                    if inside(t, NS):
                        act.wait_ge(S.pre_act, t + 1)
                        nc.scalar.activation(act_f[p][:], act_f[p][:], ACT.Silu).then_inc(S.act_ready, 1)
                        act.wait_ge(S.act_ready, t + 1)
                        after(act, S.s2_mm, t - 1)
                        nc.scalar.copy(act_hi[p][:], act_f[p][:, KF - KS:, :]).then_inc(S.act_hi_ready, 1)

                def rows(t):
                    if inside(t, NS):
                        act.wait_ge(S.x_T, t + 1)
                        after(act, S.s1_mm, t - 1)
                        for k in range(KD):
                            ins = nc.scalar.mul(xT[q][:, k, :], bk(6)[:, k * P:(k + 1) * P], rms_c[:, k:k + 1])
                        ins.then_inc(S.xT_ready, 1)
                rows(i - 1)
                silu(i - 2)
            act.wait_ge(S.tables, 1)
            act.wait_ge(S.wff_in, 16 * 2 * NE)
            pipeline(act, NS, 3, body4)

        @block.vector
        def _(dve):
            V = nc.vector
            V.memset(tab[:].bitcast(F32), 0.0).then_inc(S.tab_done, 1)
            for h in range(2):
                dve.wait_ge(S.w_emb_hi, h + 1)
                V.tensor_tensor(wemb_lo[:, h * HB:(h + 1) * HB, :].rearrange("p k d -> p (k d)"),
                                w_raw[:, h * HB * D:(h + 1) * HB * D],
                                wemb_hi[:, h * HB:(h + 1) * HB, :].rearrange("p k d -> p (k d)").bitcast(F32),
                                ALU.subtract).then_inc(S.w_emb_lo, 1)
            dve.wait_ge(S.tab_in, 96)
            for o in (0, 64):
                V.tensor_tensor(tab_raw[o:o + N, :], tab_raw[o:o + N, :], tab_add[o:o + N, :],
                                ALU.add).then_inc(S.tab_sum, 1)
            dve.wait_ge(S.tab_sum, 2)
            dve.wait_ge(S.tab_done, 1)
            V.tensor_copy(tab[0:N, :], tab_raw[0:N, :])
            V.tensor_copy(tab_tmp[64:64 + N, :], tab_raw[64:64 + N, :]).then_inc(S.tab_hi, 1)
            dve.wait_ge(S.tab_hi, 1)
            V.tensor_tensor(tab[64:64 + N, :], tab_raw[64:64 + N, :], tab_tmp[64:64 + N, :].bitcast(F32),
                            ALU.subtract).then_inc(S.tab_done, 1)

            def body(i, p):
                j = i - 1
                if inside(j, NT):
                    dve.wait_ge(S.emb_mm, j + 1)
                    V.tensor_copy(h_tok[:, bass.ds(j, 1), :].rearrange("p a d -> p (a d)"),
                                  bk(1 - p)[:, 0:D]).then_inc(S.h_ready, 1)
                    V.bn_stats(bn[1 - p][:], bk(1 - p)[:, 0:D]).then_inc(S.bn_done, 1)
                    settle(dve, S.bn_done, j + 1, S.cst_in, CST)
                    V.bn_aggr(mvt[1 - p][:], bn[1 - p][:]).then_inc(S.var_ready, 1)
                j = i - 2
                if inside(j, NT):
                    dve.wait_ge(S.std_ready, j + 1)
                    V.reciprocal(rstd[:, p:p + 1], std[:, p:p + 1]).then_inc(S.rstd_ready, 1)
                    dve.wait_ge(S.rstd_ready, j + 1)
                    dve.wait_ge(S.h_ready, j + 1)
                    after(dve, S.xhat_T, j - 1)
                    V.tensor_scalar(xhat[p][:], h_tok[:, bass.ds(j, 1), :].rearrange("p a d -> p (a d)"),
                                    mvt[p][:, 0:1], rstd[:, p:p + 1],
                                    ALU.subtract, ALU.mult).then_inc(S.xhat_ready, 1)
                j = i - 3
                if inside(j, NT):
                    dve.wait_ge(S.xn_hi_ready, j + 1)
                    V.tensor_tensor(xn_lo[:, :, bass.ds(j * P, P)],
                                    bk(3 - p)[:, 0:D].rearrange("p (k t) -> p k t", k=KD),
                                    xn_hi[:, :, bass.ds(j * P, P)].bitcast(F32), ALU.subtract).then_inc(S.xn_lo_ready, 1)
                if isinstance(i, int) and i in PIECES:
                    c = PIECES[i]
                    dve.wait_ge(S.w_hi, i - (NT - 3) + 1)
                    V.tensor_tensor(piece(wq_lo, wo_lo, c), w_raw[:, WEMB + c * KD * D:WEMB + (c + 1) * KD * D],
                                    piece(wq_hi, wo_hi, c).bitcast(F32), ALU.subtract).then_inc(S.w_split, 1)
                    if c == 3:
                        dve.wait_ge(S.w_hi, 5)
                        V.scalar_tensor_tensor(r_lo[:], rbd_raw[:], 0.25, r_hi[:].bitcast(F32), ALU.mult,
                                               ALU.subtract).then_inc(S.w_split, 1)
            pipeline(dve, NT, 3, lambda i, p: body(i, p % 2), 4, 4)

            V.tensor_scalar(blk[:], mask, -0.5 / HD, None, ALU.mult).then_inc(S.blk_done, 1)
            V.tensor_tensor(gate_rms[:], gate_sb, rms_c[:, :, None].broadcast_to([P, KD, NE]), ALU.mult).then_inc(S.gate_done, 1)
            V.tensor_copy(upper_r[:], upper)
            V.tensor_copy(ones_r[:], ones)
            V.memset(bo_split[:].bitcast(F32), 0.0).then_inc(S.bo_hi, 1)
            dve.wait_ge(S.bo_hi, 1)
            V.tensor_copy(bo_split[0:1, :], bo_raw[0:1, :])
            V.tensor_copy(bo_tmp[64:65, :], bo_raw[64:65, :]).then_inc(S.bo_hi, 1)
            dve.wait_ge(S.bo_hi, 2)
            V.tensor_tensor(bo_split[64:65, :], bo_raw[64:65, :], bo_tmp[64:65, :].bitcast(F32),
                            ALU.subtract).then_inc(S.bo_ready, 1)

            def low_part(g, pair, bias_row, hi, hi_ready, other, lo, lo_ready, free):
                dve.wait_ge(hi_ready, g + 1)
                dve.wait_ge(other, g + 1)
                after(dve, free, g)
                for m in range(KD):
                    ins = V.scalar_tensor_tensor(lo[:, m, :], bank[pair][:, m, 0:GC], b_c[:, bias_row, m:m + 1],
                                                 hi[:, m, :].bitcast(F32), ALU.add, ALU.subtract)
                ins.then_inc(lo_ready, 1)

            def mask_kv(g, p, half_i):
                dve.wait_ge(S.kv_mm, 4 * g + 2 * half_i + 2)
                after(dve, S.o_mm, g)
                for u in range(2):
                    ins = V.tensor_tensor(kv_sb[:, half_i, u, :].rearrange("p (a c) -> p a c", a=4),
                                          bk(4 + u).rearrange("p (a c) -> p a c", a=4),
                                          mask[:, None, :].broadcast_to([P, 4, P]), ALU.mult)
                ins.then_inc(S.kv_ready, 1)

            def attend(i, p):
                g, h = i, i - 1
                if inside(h, NG):
                    dve.wait_ge(S.s_copied, h + 1)
                    V.reciprocal(s_sb[:, 0, :], s_sb[:, 0, :]).then_inc(S.z_ready, 1)
                if inside(g, NG):
                    dve.wait_ge(S.v_mm, g + 1)
                    after(dve, S.pair_T, 4 * (g - 1))
                    for m in range(KD):
                        ins = V.tensor_scalar(vt[p][:, m, :, 0:N], bank[2][:, m, 0:GC].rearrange("p (b t) -> p b t", b=GI), b_c[:, 2, m:m + 1], None, ALU.add)
                    ins.then_inc(S.v_ready, 1)
                if inside(h, NG):
                    V.reciprocal(s_sb[:, 1, :], s_sb[:, 1, :]).then_inc(S.z_ready, 1)
                if inside(g, NG):
                    low_part(g, 0, 0, q_hi, S.q_hi_ready, S.sq_ready, q_lo, S.q_lo_ready, S.fq_mm)
                if inside(h, NG):
                    mask_kv(h, 1 - p, 0)
                if inside(g, NG):
                    low_part(g, 1, 1, k_hi, S.k_hi_ready, S.sk_ready, k_lo, S.k_lo_ready, S.fk_mm)
                if inside(h, NG):
                    mask_kv(h, 1 - p, 1)
                    dve.wait_ge(S.z_ready, 2 * (h + 1))
                    dve.wait_ge(S.o_mm, h + 1)
                    V.tensor_tensor(outT[:, :, bass.ds(h * GC, GC)], bank[3][:, :, 0:GC], s_sb[:],
                                    ALU.mult).then_inc(S.out_ready, 1)
            dve.wait_ge(S.tail_zero, 2)
            pipeline(dve, NG, 1, attend, 2)

            def stats(i, p):
                q = p % 2
                j = i - 1
                if inside(j, NT):
                    dve.wait_ge(S.wo_mm, j + 1)
                    V.bn_stats(bn[1 - q][:], bk(WO_BANK[(p + 3) % 4])[:, 0:D]).then_inc(S.h2_bn, 1)
                    settle(dve, S.h2_bn, j + 1, S.cst_in, CST)
                    V.bn_aggr(mvt[1 - q][:], bn[1 - q][:]).then_inc(S.h2_mv, 1)
                j = i - 2
                if inside(j, NT):
                    dve.wait_ge(S.h2_std, j + 1)
                    V.reciprocal(mvt[q][:, 1:2], std[:, q:q + 1]).then_inc(S.h2_rstd, 1)
                    dve.wait_ge(S.h2_kept, j + 1)
                    dve.wait_ge(S.h2_rstd, j + 1)
                    V.tensor_copy(mr[:, bass.ds(j, 1), :].rearrange("p a s -> p (a s)"), mvt[q][:])
                    after(dve, S.gT_mm, j - 1)
                    V.tensor_scalar(g_tok[q][:], h_tok[:, bass.ds(j, 1), :].rearrange("p a d -> p (a d)"),
                                    mvt[q][:, 0:1], mvt[q][:, 1:2],
                                    ALU.subtract, ALU.mult).then_inc(S.g_ready, 1)
            pipeline(dve, NT, 2, stats, 4, 4)

            def it(x):
                return x[:, None, :].broadcast_to([P, NE, NT])

            def ex(x):
                return x[:, :, None].broadcast_to([P, NE, NT])
            tiles_last = "p e i -> p i e"
            flat = "p e i -> p (e i)"
            done = {}

            def r(name, ins):
                done[name] = len(done) + 1
                ins.then_inc(S.rt, 1)

            def need(name):
                dve.wait_ge(S.rt, done[name])

            dve.wait_ge(S.logits_mm, NT)
            logit = bk(4)[:, 0:R]
            logit_ei = logit.rearrange("p (i e) -> p e i", e=NE)
            r("max", V.tensor_reduce(mx[:], logit.rearrange("p (i e) -> p i e", e=NE), AX.X, ALU.max))
            need("max")
            r("is_max", V.tensor_tensor(first_max[:], logit_ei, it(mx), ALU.is_equal))
            r("below", V.tensor_tensor(rt1[:], logit_ei, it(mx), ALU.subtract))
            prio = iota[:, NE:0:-1]
            need("is_max")
            r("prio", V.tensor_tensor(first_max[:], first_max[:], ex(prio), ALU.mult))
            need("prio")
            r("first", V.tensor_reduce(t19[0][:], first_max[:].rearrange(tiles_last), AX.X, ALU.max))
            need("first")
            r("onehot", V.tensor_tensor(onehot[:], it(t19[0]), ex(prio), ALU.is_equal))
            need("onehot")
            r("valid", V.tensor_scalar(onehot[:, :, NT - 1], onehot[:, :, NT - 1].bitcast(F32), valid, None, ALU.mult))
            dve.wait_ge(S.rt_act, 1)
            r("sum", V.tensor_reduce(t19[1][:], rt2[:].rearrange(tiles_last), AX.X, ALU.add))
            dve.wait_ge(S.rt_pe, 1)
            r("tot", V.tensor_copy(tot[:].rearrange("p e i -> p (e i)"), bk(6)[:, 0:R]))
            need("sum")
            r("score", V.reciprocal(t19[1][:], t19[1][:]))
            need("tot")
            r("scan", V.tensor_tensor_scan(rt1[:].rearrange(flat), unit[:], tot[:].rearrange(flat), 0.0,
                                           ALU.mult, ALU.add))
            need("score")
            r("score_valid", V.tensor_scalar(t19[1][:, NT - 1:NT], t19[1][:, NT - 1:NT], valid, None, ALU.mult))
            need("scan")
            r("before", V.tensor_tensor(tot[:], rt1[:], tot[:], ALU.subtract))
            need("score_valid")
            r("score_hi", V.tensor_copy(sc_hi[:], t19[1][:]))
            need("before")
            r("tokens", V.tensor_tensor(t8[0][:], rt1[:, :, NT - 1], tot[:, :, 0], ALU.subtract))
            need("tokens")
            r("rank", V.tensor_tensor(rt1[:].rearrange(flat), bk(5)[:, 0:R], tot[:].rearrange(flat), ALU.add))
            r("round", V.tensor_scalar(t8i[:], t8[0][:], float(P - 1), None, ALU.add))
            r("score_lo", V.tensor_tensor(t19_2[:], t19[1][:], sc_hi[:].bitcast(F32), ALU.subtract))
            need("round")
            r("shift", V.tensor_scalar(t8i[:], t8i[:], 7, None, ALU.arith_shift_right))
            need("shift")
            r("tiles", V.tensor_copy(t8[1][:], t8i[:]))
            need("tiles")
            r("ends", V.tensor_tensor_scan(t8[2][:], unit[:, 0:NE], t8[1][:], 0.0, ALU.mult, ALU.add))
            need("ends")
            r("starts", V.tensor_tensor(t8[3][:], t8[2][:], t8[1][:], ALU.subtract))
            need("starts")
            r("offset", V.scalar_tensor_tensor(t8[4][:], t8[3][:], float(P), tot[:, :, 0], ALU.mult, ALU.subtract))
            need("offset")
            r("slots", V.tensor_tensor(rt1[:], rt1[:], ex(t8[4]), ALU.add))
            need("slots")
            r("own", V.tensor_tensor(rt1[:], rt1[:], onehot[:].bitcast(F32), ALU.mult))
            need("own")
            r("slot", V.tensor_reduce(t19[3][:], rt1[:].rearrange(tiles_last), AX.X, ALU.add))
            need("slot")
            r("slot_i", V.tensor_copy(slot_i[:], t19[3][:]))
            need("slot_i")
            r("st_i", V.tensor_scalar(st_i[:], slot_i[:], 7, None, ALU.arith_shift_right))
            r("sp_i", V.tensor_scalar(sp_i[:], slot_i[:], P - 1, None, ALU.bitwise_and))
            need("st_i")
            r("st", V.tensor_copy(t19[4][:], st_i[:]))
            need("sp_i")
            r("sp", V.tensor_copy(t19[5][:], sp_i[:]))
            need("st")
            dve.wait_ge(S.h2_saved, 16 * 5)
            V.tensor_tensor(st_hot[:], iota[:, None, 0:NS].broadcast_to([P, NT, NS]),
                            t19[4][:, :, None].broadcast_to([P, NT, NS]), ALU.is_equal).then_inc(S.st_hot_ready, 1)
            need("sp")
            for a, b in ((0, NT // 2), (NT // 2, NT)):
                V.tensor_tensor(sp_hot[:, a:b, :], iota[:, None, :].broadcast_to([P, b - a, P]),
                                t19[5][:, a:b, None].broadcast_to([P, b - a, P]), ALU.is_equal).then_inc(S.hot_ready, 1)
                if a == 0:
                    dve.wait_ge(S.st_hot_ready, 1)
                    V.tensor_tensor(payload[:, :, 1, :], st_hot[:], sc_hi[:].bitcast(F32)[:, :, None].broadcast_to([P, NT, NS]),
                                    ALU.mult).then_inc(S.payload_ready, 1)
            r("passed", V.tensor_tensor(cmp26[:], iota[:, 0:NS, None].broadcast_to([P, NS, NE]),
                                        t8[2][:, None, :].broadcast_to([P, NS, NE]), ALU.is_ge))
            need("passed")
            r("e", V.tensor_reduce(t26[0][:], cmp26[:], AX.X, ALU.add))
            need("e")
            r("e_tile", V.tensor_scalar(e_tile[:], t26[0][:], float(NE - 1), None, ALU.min))
            dve.wait_ge(S.hot_mm, NT)
            V.tensor_scalar(gidx[:], bk(7)[:, 0:NS], -1.0, 0.0, ALU.add, ALU.max).then_inc(S.gather_table, 1)
            r("empty", V.tensor_scalar(t26[1][:], bk(7)[:, 0:NS], 0.0, 4096.0, ALU.is_equal, ALU.mult))
            r("score_part", V.tensor_copy(t26[2][:], bk(7)[:, NS:2 * NS]))
            need("empty")
            r("sidx", V.scalar_tensor_tensor(sidx[:], bk(7)[:, 0:NS], -1.0, t26[1][:], ALU.add, ALU.add))
            need("score_part")
            V.tensor_tensor(slot_score[:], bk(7)[:, 2 * NS:3 * NS], t26[2][:], ALU.add).then_inc(S.tables, 1)

            def body4(i, p):
                q = 1 - p
                t = i - 1
                if inside(t, NS):
                    e = dve.value_load(e_tile[0:1, bass.ds(t, 1)], min_val=0, max_val=NE - 1)
                    after(dve, S.s1_mm, t - 1)
                    V.tensor_copy(w1_s[q][:, 1, :], wff[:, bass.ds(e, 1), FF:2 * FF].rearrange("p a n -> p (a n)")).then_inc(S.w1_b, 1)
                t = i - 2
                if inside(t, NS):
                    e = dve.value_load(e_tile[0:1, bass.ds(t, 1)], min_val=0, max_val=NE - 1)
                    dve.wait_ge(S.s1_mm, t + 1)
                    after(dve, S.s2_mm, t - 1)
                    V.tensor_tensor(act_f[p][:], bank[p][:].rearrange("p a (b t) -> p (a b) t", t=P),
                                    b1_c[:, bass.ds(e, 1), :].rearrange("p a k -> p (a k)")[:, :, None].broadcast_to([P, KF, P]),
                                    ALU.add).then_inc(S.pre_act, 1)
                    dve.wait_ge(S.w2_hi_ready, t + 1)
                    V.tensor_tensor(w2_lo[p][:].rearrange("p k d -> p (k d)"),
                                    wff[:, bass.ds(e, 1), W2S:].rearrange("p a n -> p (a n)"),
                                    w2_hi[p][:].rearrange("p k d -> p (k d)").bitcast(F32), ALU.subtract).then_inc(S.w2_lo_ready, 1)
                    dve.wait_ge(S.row_copied, t + 1)
                    V.scalar_tensor_tensor(h2c[p][:], b2_bc[:, bass.ds(e, 1), :].rearrange("p a d -> p (a d)"),
                                           slot_score[:, bass.ds(t, 1)], h2c[p][:], ALU.mult, ALU.add).then_inc(S.b2_added, 1)
                t = i - 3
                if inside(t, NS):
                    dve.wait_ge(S.s2_mm, t + 1)
                    dve.wait_ge(S.b2_added, t + 1)
                    after(dve, S.o_saved, 16 * t)
                    V.scalar_tensor_tensor(o_sb[:], bk(7)[:, 0:D], slot_score[:, bass.ds(t, 1)], h2c[q][:],
                                           ALU.mult, ALU.add).then_inc(S.o_ready, 1)
                t = i - 1
                if inside(t, NS):
                    dve.wait_ge(row_in[q], 16 * (t // 2 + 1))
                    after(dve, S.o_ready, t - 1)
                    V.tensor_copy(h2c[q][:], row[q][:, 0:D]).then_inc(S.row_copied, 1)
                if inside(i, NS):
                    dve.wait_ge(row_in[p], 16 * (i // 2 + 1))
                    after(dve, S.x_T, i)
                    V.tensor_scalar(x_sb[:], row[p][:, 0:D], row[p][:, D:D + 1], row[p][:, D + 1:D + 2],
                                    ALU.subtract, ALU.mult).then_inc(S.x_ready, 1)
            dve.wait_ge(S.tables, 1)
            dve.wait_ge(S.wff_in, 16 * 2 * NE)
            dve.wait_ge(S.bias_in, 16)
            pipeline(dve, NS, 3, body4)

        @block.tensor
        def _(pe):
            def mm(o, lhsT, rhs, first, last):
                return nc.tensor.matmul(o, lhsT, rhs, start=first, stop=last, skip_group_check=True)

            def mm3(o, w, x, first, last):
                mm(o, w[1], x[0], first, False)
                mm(o, w[0], x[1], False, False)
                return mm(o, w[0], x[0], False, last)


            def project(g, which, pair):
                for m in range(KD):
                    for k in range(KD):
                        ins = mm3(bank[pair][:, m, 0:GC],
                                  (wq_hi[:, which, k, m * P:(m + 1) * P], wq_lo[:, which, k, m * P:(m + 1) * P]),
                                  (xn_hi[:, k, bass.ds(g * GC, GC)], xn_lo[:, k, bass.ds(g * GC, GC)]),
                                  k == 0, k == KD - 1)
                return ins

            def stage1(i, p):
                if inside(i, NT):
                    after(pe, S.h_ready, i - 1)
                    after(pe, S.bn_done, i - 1)
                    for k in range(KP):
                        if k % HB == 0:
                            pe.wait_ge(S.x_lo_ready, 2 * i + k // HB + 1)
                            if isinstance(i, int) and i == 0:
                                pe.wait_ge(S.w_emb_lo, k // HB + 1)
                        ins = mm3(bk(p)[:, 0:D], (x_hi[p][:, k, :], x_lo[p][:, k, :]),
                                  (wemb_hi[:, k, :], wemb_lo[:, k, :]), k == 0, False)
                        if k == HB - 1:
                            ins.then_inc(S.emb_half, 1)
                    if isinstance(i, int) and i == 0:
                        pe.wait_ge(S.tab_done, 2)
                    mm(bk(p)[:, 0:D], x_hi[p][:, KP, :], tab[:], False, True).then_inc(S.emb_mm, 1)
                if isinstance(i, int) and i == NT:
                    pe.wait_ge(S.w_split, 1)
                    pe.wait_ge(S.xn_lo_ready, -(-GC // P))
                    project(0, 2, 2).then_inc(S.v_mm, 1)
                if isinstance(i, int) and i == NT + 1:
                    pe.wait_ge(S.w_split, 2)
                    pe.wait_ge(S.bn_done, NT)
                    project(0, 0, 0).then_inc(S.q_mm, 1)
                j = i - 2
                if isinstance(j, int) and j == 0:
                    pe.wait_ge(S.cst_in, CST)
                if inside(j, NT):
                    pe.wait_ge(S.xhat_ready, j + 1)
                    after(pe, S.xn_lo_ready, j - 1)
                    for k in range(KD):
                        ins = nc.tensor.transpose(bk(2 + p)[:, k * P:(k + 1) * P], xhat[p][:, k * P:(k + 1) * P], ident)
                    ins.then_inc(S.xhat_T, 1)
            pipeline(pe, NT, 2, stage1)

            def feature(pair, hi, lo, sq, between=None):
                for m in range(KD):
                    o = bank[pair][:, m, 0:GC]
                    for n, (w, x) in enumerate(((r_lo, hi), (r_hi, lo), (r_hi, hi), (blk, sq))):
                        ins = mm(o, w[:], x[:, m, :], n == 0, n == 3)
                        if between:
                            between(4 * m + n)
                return ins

            def output(h, ph, n):
                b, m = n // KD, n % KD
                if n == 0:
                    pe.wait_ge(S.kv_ready, 2 * h + 1)
                    pe.wait_ge(S.pair_ready, 4 * h + 4)
                if n == GI:
                    pe.wait_ge(S.kv_ready, 2 * h + 2)
                c = (b // 2 % 2) * 2 * P + m * P
                return mm(bk(6 + m)[:, b * N:(b + 1) * N], kv_sb[:, b // 4, b % 2, c:c + P],
                          qp[ph][:, m, b * N:(b + 1) * N], True, True)

            def pair_T(g, p, j):
                pe.wait_ge(S.kp_ready, g + 1)
                pe.wait_ge(S.v_ready, g + 1)
                after(pe, S.pair_ready, 4 * g + j - 1)
                if j < 2:
                    after(pe, S.out_ready, g)
                o = bk(6 + j % 2)
                for c, buf in enumerate((vt[p], kp[p])):
                    for m in range(KD):
                        ins = nc.tensor.transpose(o[:, (2 * c + m) * P:(2 * c + m + 1) * P], buf[:, m, 2 * j:2 * j + 2, :].rearrange("p b t -> p (b t)"),
                                                  ident)
                ins.then_inc(S.pair_T, 1)

            def pair_kv(g, j):
                pe.wait_ge(S.pair_ready, 4 * g + j + 1)
                if j == 2:
                    pe.wait_ge(S.kv_ready, 2 * g + 1)
                for u in range(2):
                    for m in range(KD):
                        ins = mm(bk(4 + u)[:, ((j % 2) * 2 + m) * P:((j % 2) * 2 + m + 1) * P],
                                 kv_t[j % 2][64 * u:64 * u + N, (2 + m) * P:(3 + m) * P],
                                 kv_t[j % 2][64 * u:64 * u + N, m * P:(m + 1) * P], True, True)
                ins.then_inc(S.kv_mm, 1)

            def residual(i, p):
                q = p % 2
                if inside(i, NT):
                    after(pe, S.h2_kept, i - 3)
                    o = bk(WO_BANK[p])[:, 0:D]
                    mm(o, ident, h_tok[:, bass.ds(i, 1), :].rearrange("p a d -> p (a d)"), True, False)
                    mm(o, ones_r[:], bo_split[:], False, False)
                    pe.wait_ge(S.ol_ready, i + 1)
                    for m in range(KD):
                        ins = mm3(o, (oh[p][:, m, :], ol[p][:, m, :]), (wo_hi[:, m, :], wo_lo[:, m, :]),
                                  False, m == KD - 1)
                    ins.then_inc(S.wo_mm, 1)
                j = i - 2
                if inside(j, NT):
                    pe.wait_ge(S.g_ready, j + 1)
                    after(pe, S.gT_ready, j - 1)
                    for k in range(KD):
                        ins = nc.tensor.transpose(bk(2 + q)[:, k * P:(k + 1) * P], g_tok[q][:, k * P:(k + 1) * P], ident)
                    ins.then_inc(S.gT_mm, 1)
                j = i - 3
                if inside(j, NT):
                    pe.wait_ge(S.gT_ready, j + 1)
                    for k in range(KD):
                        ins = mm(bk(4)[:, bass.ds(j * NE, NE)], gT[1 - q][:, k, :], gate_rms[:, k, :], k == 0, k == KD - 1)
                    ins.then_inc(S.logits_mm, 1)
            def attend(i, p):
                g, h, ph = i, i - 1, 1 - p
                if inside(h, NG):
                    pe.wait_ge(S.qp_ready, h + 1)
                    after(pe, S.kv_ready, 2 * h)
                    for m in range(KD):
                        ins = mm(bk(4 + m)[:, 0:GC], blk[:], qp[ph][:, m, :], True, True)
                    ins.then_inc(S.s_mm, 1)
                if isinstance(i, int) and i == NG:
                    pe.wait_ge(S.bo_ready, 1)
                    residual(0, 0)
                if inside(g, NG) and not (isinstance(g, int) and g == 0):
                    pe.wait_ge(S.qp_ready, g)
                    project(g, 0, 0).then_inc(S.q_mm, 1)
                if inside(h, NG):
                    pair_T(h, ph, 0)
                    pair_T(h, ph, 1)
                if inside(g, NG) and not (isinstance(g, int) and g == 0):
                    pe.wait_ge(S.s_copied, g)
                    project(g, 2, 2).then_inc(S.v_mm, 1)
                if inside(g, NG):
                    if isinstance(g, int) and g == 0:
                        pe.wait_ge(S.xn_lo_ready, NT)
                    after(pe, S.kp_ready, g)
                    project(g, 1, 1).then_inc(S.k_mm, 1)
                if inside(h, NG):
                    if inside(g, NG):
                        pe.wait_ge(S.v_ready, g + 1)
                    else:
                        pe.wait_ge(S.s_copied, h + 1)
                    pair_kv(h, 0)
                    pair_kv(h, 1)
                    pair_T(h, ph, 2)
                    pair_T(h, ph, 3)
                if inside(g, NG):
                    pe.wait_ge(S.q_lo_ready, g + 1)
                    feature(0, q_hi, q_lo, s_q).then_inc(S.fq_mm, 1)
                if inside(h, NG):
                    pair_kv(h, 2)
                    pair_kv(h, 3)
                first_half = (lambda n: output(h, ph, n)) if inside(h, NG) else None
                if inside(g, NG):
                    pe.wait_ge(S.k_lo_ready, g + 1)
                    feature(1, k_hi, k_lo, s_k, first_half).then_inc(S.fk_mm, 1)
                else:
                    residual(1, 1)
                    for n in range(GI):
                        first_half(n)
                if inside(h, NG):
                    for n in range(GI, KD * GI):
                        ins = output(h, ph, n)
                    ins.then_inc(S.o_mm, 1)
            pe.wait_ge(S.w_split, 5)
            pe.wait_ge(S.blk_done, 1)
            pipeline(pe, NG, 1, attend, 2)

            pe.wait_ge(S.gate_done, 1)
            pe.wait_ge(S.out_ready, NG)
            pipeline(pe, NT, 3, residual, 4, 4, start=2)

            pe.wait_ge(S.rt, 7)
            mm(bk(5)[:, 0:R], upper_r[:], onehot[:].rearrange("p e i -> p (e i)"), True, True)
            mm(bk(6)[:, 0:R], ones_r[:], onehot[:].rearrange("p e i -> p (e i)"), True, True).then_inc(S.rt_pe, 1)
            pe.wait_ge(S.payload_ready, 1)
            pe.wait_ge(S.payload_pool, 2)
            for i in range(NT):
                if i in (0, NT // 2):
                    pe.wait_ge(S.hot_ready, 1 if i == 0 else 2)
                mm(bk(7)[:, 0:3 * NS], sp_hot[:, i, :], payload[:, i, :, :].rearrange("p c s -> p (c s)"),
                   i == 0, i == NT - 1).then_inc(S.hot_mm, 1)

            def x_T(t, p):
                pe.wait_ge(S.x_ready, t + 1)
                after(pe, S.xT_ready, t)
                for k in range(KD):
                    ins = nc.tensor.transpose(bk(6)[:, k * P:(k + 1) * P], x_sb[:, k * P:(k + 1) * P], ident)
                ins.then_inc(S.x_T, 1)

            def body4(i, p):
                q = 1 - p
                if isinstance(i, int) and i == 2:
                    x_T(1, 1)
                t = i - 2
                if inside(t, NS):
                    pe.wait_ge(S.xT_ready, t + 1)
                    pe.wait_ge(S.w1_a, t + 1)
                    pe.wait_ge(S.w1_b, t + 1)
                    after(pe, S.pre_act, t - 1)
                    for f in range(KF):
                        for k in range(KD):
                            ins = mm(bank[p][:, f // 4, f % 4 * P:(f % 4 + 1) * P], w1_s[p][:, k, f * P:(f + 1) * P],
                                     xT[p][:, k, :], k == 0, k == KD - 1)
                    ins.then_inc(S.s1_mm, 1)
                if inside(i - 1, NS) and not (isinstance(i, int) and i == 2):
                    x_T(i - 1, q)
                t = i - 3
                if inside(t, NS):
                    e = pe.value_load(e_tile[0:1, bass.ds(t, 1)], min_val=0, max_val=NE - 1)
                    after(pe, S.o_ready, t)
                    pe.wait_ge(S.act_ready, t + 1)
                    for k in range(KF - KS):
                        c = KD * FF + k * D
                        mm(bk(7)[:, 0:D], act_f[q][:, k, :], wff[:, bass.ds(e, 1), c:c + D].rearrange("p a n -> p (a n)"),
                           k == 0, False)
                    pe.wait_ge(S.w2_lo_ready, t + 1)
                    pe.wait_ge(S.act_lo_ready, t + 1)
                    for k in range(KS):
                        ins = mm3(bk(7)[:, 0:D], (act_hi[q][:, k, :], act_lo[q][:, k, :]),
                                  (w2_hi[q][:, k, :], w2_lo[q][:, k, :]), False, k == KS - 1)
                    ins.then_inc(S.s2_mm, 1)
            pe.wait_ge(S.tables, 1)
            pipeline(pe, NS, 3, body4)


def kernel(**inputs):
    import numpy as np
    import concourse.bacc as bacc
    from concourse.bass_utils import run_bass_kernel_spmd

    f = np.float32

    def blocks(w):
        k, m = w.shape
        return np.ascontiguousarray(w.reshape(k // P, P, m).transpose(1, 0, 2).reshape(P, -1))

    x = np.asarray(inputs["x"])
    patches = np.zeros((PIX, IMGS, N), x.dtype)
    patches[:, :, 1:] = x.reshape(IMGS, 3, 6, 16, 6, 16).transpose(1, 3, 5, 0, 2, 4).reshape(PIX, IMGS, N - 1)
    xin = np.zeros((NT, P, KP + 1, P), x.dtype)
    cols = np.zeros((PIX, NT * P), x.dtype)
    cols[:, :T] = patches.reshape(PIX, T)
    xin[:, :, :KP, :] = cols.reshape(KP, P, NT, P).transpose(2, 1, 0, 3)
    tok = np.arange(NT * P) % N
    sel = np.zeros((P, NT * P), f)
    sel[tok, np.arange(NT * P)] = 1
    sel[64 + tok, np.arange(NT * P)] = 1
    xin[:, :, KP, :] = sel.reshape(P, NT, P).transpose(1, 0, 2)

    w_all = np.concatenate([blocks(np.asarray(inputs[n]).T) for n in
                            ("L0_tok_W", "L0_attn_Wq", "L0_attn_Wk", "L0_attn_Wv", "L0_attn_Wo")], axis=1)
    head = np.arange(P) // HD
    consts = np.concatenate([
        np.eye(P, dtype=f), (head[:, None] == head[None, :]).astype(f),
        (np.arange(P)[:, None] < np.arange(P)[None, :]).astype(f), np.ones((P, P), f),
        np.tile(np.arange(P, dtype=f), (P, 1)),
        np.tile((np.arange(P) < T - (NT - 1) * P).astype(f)[:, None], (1, 2))], axis=1)
    number = np.arange(NT * P).reshape(NT, P).T
    ids = np.where(number < T, number + 1, 0).astype(f)
    small = np.concatenate([np.asarray(inputs[n]).reshape(KD, P).T for n in
                            ("L0_attn_bq", "L0_attn_bk", "L0_attn_bv", "L0_ffn_rms_w")]
                           + [blocks(np.asarray(inputs["L0_ffn_gate_w"]).T)], axis=1)
    arrays = {
        "xin": xin, "w_all": w_all, "Rm": inputs["L0_attn_R"], "tok_b": inputs["L0_tok_b"],
        "cls_tok": inputs["L0_tok_class_token"], "pos": inputs["L0_tok_pos_embedding"],
        "small": small, "bo": inputs["L0_attn_bo"],
        "W1": inputs["L0_ffn_W1"], "b1": np.asarray(inputs["L0_ffn_b1"]).reshape(NE, KF, P).transpose(2, 0, 1), "W2": inputs["L0_ffn_W2"], "b2": inputs["L0_ffn_b2"],
        "consts": consts, "ids": ids,
    }
    arrays = {k: np.ascontiguousarray(v) for k, v in arrays.items()}
    nc = bacc.Bacc("TRN2", target_bir_lowering=False, num_devices=1)
    args = [nc.dram_tensor(k, v.shape, mybir.dt.from_np(v.dtype), kind="ExternalInput").ap() for k, v in arrays.items()]
    out = nc.dram_tensor("out", (IMGS, N, D), F32, kind="ExternalOutput").ap()
    vit_kernel(nc, *args, out)
    r = run_bass_kernel_spmd(nc, [arrays], core_ids=[0])
    return r.results[0]["out"]
```
